# Optimizing a Trainium2 kernel written in Bass

```python
import numpy as np
import jax
import jax.numpy as jnp

def _softmax(x, axis=-1):
    return jax.nn.softmax(x, axis=axis)

def _gelu(x):
    return jax.nn.gelu(x, approximate=True)

def _silu(x):
    return jax.nn.silu(x)

def _sigmoid(x):
    return jax.nn.sigmoid(x)

def _layernorm(x, axis=-1, eps=1e-05):
    m = jnp.mean(x, axis=axis, keepdims=True)
    v = jnp.var(x, axis=axis, keepdims=True)
    return (x - m) / jnp.sqrt(v + eps)

def _scatter_add(tgt, idx, src, axis=0):
    return tgt.at[idx].add(src)

def _segment_sum(src, seg, n):
    return jax.ops.segment_sum(src, seg, n)
kernel_name = 'mk_adj_ffn_d1_adj_r2_904bc1'

def setup_inputs(seed: int=0):
    np.random.seed(seed)
    _w = jnp.asarray

    def _rec_inputs():
        import jax
        import jax.numpy as jnp
        _gk = jax.random.key(seed)
        x = -0.0002928 + 1 * jax.random.normal(jax.random.fold_in(_gk, 1), (128, 128, 128), jnp.float32)
        _a = jax.random.bernoulli(jax.random.fold_in(_gk, 2), 0.0625, (128, 128, 128))
        adj = _a
        return (x, adj)
    x, adj = _rec_inputs()

    def _L0_gnn_setup():
        import jax, jax.numpy as jnp
        import numpy as np
        B, L, CIN, COUT, HEADS = (8, 1024, 128, 128, 4)
        HD = COUT // HEADS
        NEG_SLOPE = 0.2
        key = jax.random.key(seed)
        k1, k2, k3, k4, k5 = jax.random.split(key, 5)
        x = jax.random.normal(k1, (B, L, CIN), dtype=jnp.float32)
        adj_mask = jax.random.randint(k2, (B, L, L), 0, 2) > 0
        W = jax.random.normal(k3, (COUT, CIN), dtype=jnp.float32) * (1.0 / np.sqrt(CIN))
        att_src = jax.random.normal(k4, (1, HEADS, 1, HD), dtype=jnp.float32) * 0.1
        att_dst = jax.random.normal(k5, (1, HEADS, 1, HD), dtype=jnp.float32) * 0.1
        return {'x': x, 'adj_mask': adj_mask, 'W': W, 'att_src': att_src, 'att_dst': att_dst}
    _L0_gnn_all = _L0_gnn_setup()
    _L0_gnn_in = {k: v for k, v in _L0_gnn_all.items() if k in ('W', 'att_src', 'att_dst')}
    del _L0_gnn_all

    def _L0_ffn_setup():
        import jax, jax.numpy as jnp
        import numpy as np
        B, T, C = (64, 192, 128)
        NH, NKV = (4, 2)
        HD = C // NH
        NREP = NH // NKV
        NE, TOPK = (8, 2)
        HID = int(8 / 3 * C)
        EPS_RMS = 1e-06

        def _rope_tables(t_len):
            inv_freq = 1.0 / 10000.0 ** (np.arange(0, HD, 2, dtype=np.float32) / HD)
            t = np.arange(t_len, dtype=np.float32)
            freqs = np.outer(t, inv_freq)
            emb = np.concatenate([freqs, freqs], axis=-1)
            return (jnp.asarray(np.cos(emb)), jnp.asarray(np.sin(emb)))

        def _rotate_half(x):
            h = x.shape[-1] // 2
            return jnp.concatenate([-x[..., h:], x[..., :h]], axis=-1)

        def _rmsnorm(v, w):
            return v * jax.lax.rsqrt(jnp.mean(v * v, axis=-1, keepdims=True) + EPS_RMS) * w
        key = jax.random.key(seed)
        ks = jax.random.split(key, 10)
        s = lambda k, shape: jax.random.normal(k, shape, jnp.float32) * 0.02
        return {'x': jax.random.normal(ks[0], (B, T, C), jnp.float32), 'ln1_w': jnp.ones((C,), jnp.float32), 'ln2_w': jnp.ones((C,), jnp.float32), 'wq': s(ks[1], (NH * HD, C)), 'wk': s(ks[2], (NKV * HD, C)), 'wv': s(ks[3], (NKV * HD, C)), 'wo': s(ks[4], (C, C)), 'router_w': s(ks[5], (NE, C)), 'w1': s(ks[6], (NE, HID, C)), 'w2': s(ks[7], (NE, C, HID)), 'w3': s(ks[8], (NE, HID, C))}
    _L0_ffn_all = _L0_ffn_setup()
    _L0_ffn_in = {k: v for k, v in _L0_ffn_all.items() if k in ('ln1_w', 'ln2_w', 'wq', 'wk', 'wv', 'wo', 'router_w', 'w1', 'w2', 'w3')}
    del _L0_ffn_all
    return {'x': x, 'adj': adj, 'L0_gnn_W': _L0_gnn_in['W'], 'L0_gnn_att_src': _L0_gnn_in['att_src'], 'L0_gnn_att_dst': _L0_gnn_in['att_dst'], 'L0_ffn_ln1_w': _L0_ffn_in['ln1_w'], 'L0_ffn_ln2_w': _L0_ffn_in['ln2_w'], 'L0_ffn_wq': _L0_ffn_in['wq'], 'L0_ffn_wk': _L0_ffn_in['wk'], 'L0_ffn_wv': _L0_ffn_in['wv'], 'L0_ffn_wo': _L0_ffn_in['wo'], 'L0_ffn_router_w': _L0_ffn_in['router_w'], 'L0_ffn_w1': _L0_ffn_in['w1'], 'L0_ffn_w2': _L0_ffn_in['w2'], 'L0_ffn_w3': _L0_ffn_in['w3']}

def reference(x, adj, L0_gnn_W, L0_gnn_att_src, L0_gnn_att_dst, L0_ffn_ln1_w, L0_ffn_ln2_w, L0_ffn_wq, L0_ffn_wk, L0_ffn_wv, L0_ffn_wo, L0_ffn_router_w, L0_ffn_w1, L0_ffn_w2, L0_ffn_w3):
    import jax
    import jax.numpy as jnp

    def _L0_gnn_ref(x, adj_mask, W, att_src, att_dst):
        import jax, jax.numpy as jnp
        import numpy as np
        B, L, CIN, COUT, HEADS = (8, 1024, 128, 128, 4)
        HD = COUT // HEADS
        NEG_SLOPE = 0.2
        Bb, Ll, _ = x.shape
        h = jnp.einsum('blc,oc->blo', x, W).reshape(Bb, Ll, HEADS, HD).transpose(0, 2, 1, 3)
        a_src = jnp.sum(h * att_src, axis=-1, keepdims=True)
        a_dst = jnp.sum(h * att_dst, axis=-1, keepdims=True)
        e = a_src + jnp.swapaxes(a_dst, 2, 3)
        e = jnp.where(e >= 0, e, NEG_SLOPE * e)
        fill = jnp.finfo(e.dtype).min
        e = jnp.where(adj_mask[:, None, :, :], e, fill)
        alpha = jax.nn.softmax(e, axis=-1)
        out = jnp.einsum('bhij,bhjd->bhid', alpha, h)
        return out.transpose(0, 2, 1, 3).reshape(Bb, Ll, COUT)

    def _L0_ffn_ref(x, ln1_w, ln2_w, wq, wk, wv, wo, router_w, w1, w2, w3):
        import jax, jax.numpy as jnp
        import numpy as np
        B, T, C = (64, 192, 128)
        NH, NKV = (4, 2)
        HD = C // NH
        NREP = NH // NKV
        NE, TOPK = (8, 2)
        HID = int(8 / 3 * C)
        EPS_RMS = 1e-06

        def _rope_tables(t_len):
            inv_freq = 1.0 / 10000.0 ** (np.arange(0, HD, 2, dtype=np.float32) / HD)
            t = np.arange(t_len, dtype=np.float32)
            freqs = np.outer(t, inv_freq)
            emb = np.concatenate([freqs, freqs], axis=-1)
            return (jnp.asarray(np.cos(emb)), jnp.asarray(np.sin(emb)))

        def _rotate_half(x):
            h = x.shape[-1] // 2
            return jnp.concatenate([-x[..., h:], x[..., :h]], axis=-1)

        def _rmsnorm(v, w):
            return v * jax.lax.rsqrt(jnp.mean(v * v, axis=-1, keepdims=True) + EPS_RMS) * w
        Bx, Tx, Cx = x.shape
        h = _rmsnorm(x, ln1_w)
        q = (h @ wq.T).reshape(Bx, Tx, NH, HD).transpose(0, 2, 1, 3)
        k = (h @ wk.T).reshape(Bx, Tx, NKV, HD).transpose(0, 2, 1, 3)
        v = (h @ wv.T).reshape(Bx, Tx, NKV, HD).transpose(0, 2, 1, 3)
        cos, sin = _rope_tables(Tx)
        cos, sin = (cos[None, None], sin[None, None])
        q = q * cos + _rotate_half(q) * sin
        k = k * cos + _rotate_half(k) * sin
        k = jnp.repeat(k, NREP, axis=1)
        v = jnp.repeat(v, NREP, axis=1)
        scores = jnp.einsum('bhtd,bhsd->bhts', q, k) / jnp.sqrt(jnp.float32(HD))
        causal = jnp.tril(jnp.ones((Tx, Tx), dtype=bool))
        scores = jnp.where(causal[None, None], scores, jnp.float32(-1e+30))
        att = jax.nn.softmax(scores, axis=-1)
        y = jnp.einsum('bhts,bhsd->bhtd', att, v).transpose(0, 2, 1, 3).reshape(Bx, Tx, Cx)
        x = x + y @ wo.T
        flat = _rmsnorm(x, ln2_w).reshape(-1, Cx)
        probs = jax.nn.softmax(flat @ router_w.T, axis=-1)
        tp, ti = jax.lax.top_k(probs, TOPK)
        tp = tp / (jnp.sum(tp, axis=-1, keepdims=True) + 1e-09)
        weights = jnp.sum(tp[..., None] * jax.nn.one_hot(ti, NE, dtype=flat.dtype), axis=1)
        out = jnp.zeros_like(flat)
        for e in range(NE):
            hh = jax.nn.silu(flat @ w1[e].T) * (flat @ w3[e].T)
            out = out + weights[:, e:e + 1] * (hh @ w2[e].T)
        return x + out.reshape(Bx, Tx, Cx)
    x = x + _L0_gnn_ref(_layernorm(x, axis=-1), adj, L0_gnn_W, L0_gnn_att_src, L0_gnn_att_dst)
    x = x + _L0_ffn_ref(_layernorm(x, axis=-1), L0_ffn_ln1_w, L0_ffn_ln2_w, L0_ffn_wq, L0_ffn_wk, L0_ffn_wv, L0_ffn_wo, L0_ffn_router_w, L0_ffn_w1, L0_ffn_w2, L0_ffn_w3)
    return x

_drawn_inputs = setup_inputs


def setup_inputs(seed=0):
    import zlib

    import numpy as np

    out = dict(_drawn_inputs(seed))
    spreads = {'L0_ffn_ln1_w': (1.0, 0.6), 'L0_ffn_ln2_w': (1.0, 0.6)}
    factors = {'L0_ffn_wq': 8.0,
     'L0_ffn_wk': 8.0,
     'L0_ffn_wv': 8.0,
     'L0_ffn_wo': 8.0,
     'L0_ffn_router_w': 8.0,
     'L0_ffn_w1': 8.0,
     'L0_ffn_w2': 8.0,
     'L0_ffn_w3': 8.0}
    for name, (base, spread) in spreads.items():
        noise = np.random.default_rng([zlib.crc32(name.encode()), seed]).standard_normal(out[name].shape)
        drawn = base * np.exp(spread * noise) if base else spread * noise
        out[name] = jnp.asarray(drawn.astype(out[name].dtype))
    for name, factor in factors.items():
        out[name] = (out[name] * factor).astype(out[name].dtype)
    return out
```

```python
from contextlib import ExitStack

import numpy as np
import concourse.bass as bass
from concourse import mybir
from concourse.alu_op_type import AluOpType as ALU

F32 = mybir.dt.float32
BF16 = mybir.dt.bfloat16
U8 = mybir.dt.uint8
U32 = mybir.dt.uint32
I32 = mybir.dt.int32
ACT = mybir.ActivationFunctionType
AX = mybir.AxisListType

B, L, C = 128, 128, 128
NH, HD = 4, 32
NE, HID = 8, 341
GB = 4
NG = B // GB
GW, HW = HD + 2, HD + 1
SKEW = HD - 1
HC = [(0, 128), (128, 128), (256, HID - 256)]
ROW = C + 2
REGION = B + 1
NT = 2 * B + NE
TOK = B * L
BIG = float(2.0 ** 100)
EPS_LN, EPS_RMS, EPS_TOP = 1e-5, 1e-6, 1e-9
ROUTE = 28


def tables():
    inv = (1.0 / 10000.0 ** (np.arange(0, HD, 2, dtype=np.float32) / HD)).astype(np.float32)
    fr = np.outer(np.arange(L, dtype=np.float32), inv)
    emb = np.concatenate([fr, fr], -1)
    cos, sin = np.cos(emb).T.astype(np.float32), np.sin(emb).T.astype(np.float32)
    sin = np.concatenate([-sin[:HD // 2], sin[HD // 2:]])
    cos, sin = np.tile(cos, (NH, 1)), np.tile(sin, (NH, 1))
    scale = np.float32(1.0) / np.sqrt(np.float32(HD))
    rope = np.stack([cos * scale, sin * scale, cos, sin], 1).astype(np.float32)
    p = np.arange(128, dtype=np.float32)
    small = np.zeros((128, 3 * NE + 1 + 2 * GB), np.float32)
    small[:, 0:NE] = np.arange(NE)
    small[:, NE:2 * NE] = np.arange(NE) * REGION * L
    small[:, 2 * NE] = p
    first = np.arange(2)[:, None] * TOK + np.arange(GB)[None] * L
    small[:, 3 * NE + 1:] = p[:, None] + first.reshape(1, -1) - GB * L
    return {"rope": rope.reshape(128, 4 * L), "ident": np.eye(128, dtype=np.float32),
            "causal": np.where(np.tril(np.ones((L, L), bool)), 0.0, -BIG).astype(np.float32),
            "before": (p[:, None] < p[None]).astype(np.float32), "small": small,
            "tileno": np.arange(NT, dtype=np.float32)[None]}


def gnn_moe_block(nc, x, adj, W, WT, att_src, att_dst, ln1, ln2, wq, wqr, wk, wkr, wv, wo, router,
                  w1, w3, w2, rope_h, ident_h, causal_h, before_h, small_h, tileno_h, out):
    ctx = ExitStack()
    with ctx:
        def sb(name, shape, dt=F32):
            return ctx.enter_context(nc.sbuf_tensor(name, shape, dt))

        def sem(name):
            return ctx.enter_context(nc.semaphore(name))

        def two(name, shape, dt=F32):
            return [sb(f"{name}{i}", shape, dt) for i in range(2)]

        def dram(name, shape):
            return nc.dram_tensor(name, shape, F32, kind="Internal").ap()

        routed = dram("routed", [(NE * REGION + NE) * L, ROW])
        parts = dram("parts", [2 * TOK + 2 * NE * L, C])
        base_d = dram("base_d", [TOK, C])

        ident = sb("ident", [128, 128])
        identb = sb("identb", [128, 128], BF16)
        tmp_f = sb("tmp_f", [128, 2, 128])
        causal = sb("causal", [128, 128], BF16)
        before = sb("before", [128, 128], BF16)
        onesb = sb("onesb", [128, 128], BF16)
        rope = sb("rope", [128, 4, L])
        small = sb("small", [128, 3 * NE + 1 + 2 * GB])
        expno, region0, partno = small[:, 0:NE], small[:, NE:2 * NE], small[:, 2 * NE:2 * NE + 1]
        tileno = sb("tileno", [1, NT])
        ln1c = sb("ln1c", [C, 1])
        ln2c = sb("ln2c", [C, 1])
        half = sb("half", [128, GB])
        w_oc = sb("w_oc", [C, C])
        att = sb("att", [C, 2 * NH])
        wh = sb("wh", [C, NH, HD + 1])
        wd = sb("wd", [C, NH, L])
        projw = sb("projw", [C, 4, C])
        wv_s = sb("wv_s", [C, C])
        wo_s = sb("wo_s", [C, C])
        rout = sb("rout", [C, 128])
        w1_s = sb("w1_s", [C, NE, HID])
        w3_s = sb("w3_s", [C, NE, HID])
        w2_s = sb("w2_s", [128, NE, 3, C])

        xs = two("xs", [L, GB, C])
        adj8 = two("adj8", [L, GB, L], U8)
        mask = sb("mask", [L, GB, L], BF16)
        st_g, mv_g = sb("st_g", [L, GB, 6]), sb("mv_g", [L, GB, 2])
        ve_g, rstd = sb("ve_g", [L, GB]), sb("rstd", [L, GB])
        xn, xnT = sb("xn", [L, GB, C]), sb("xnT", [C, GB, L])
        hE = sb("hE", [L, GB, NH * GW + 1])
        tb, ub = sb("tb", [L, NH, L]), two("ub", [L, NH, L])
        nm1 = sb("nm1", [L, GB, NH])
        p1, pT1 = two("p1", [L, NH, L]), two("pT1", [L, NH, L])
        ri1, og = sb("ri1", [L, GB, NH]), sb("og", [L, GB, C])
        x1 = two("x1", [L, GB, C])
        st_a, mv_a = sb("st_a", [L, GB, 6]), sb("mv_a", [L, GB, 2])
        va, r1, r2, r12 = sb("va", [L, 4, GB]), sb("r1", [L, GB]), sb("r2", [L, GB]), sb("r12", [L, GB])
        z, hN, hT = two("z", [L, GB, C]), sb("hN", [L, GB, C]), sb("hT", [C, GB, L])
        qa, qb, qT = sb("qa", [C, GB, L]), sb("qb", [C, GB, L]), sb("qT", [C, GB, L])
        ka, kb, kk = sb("ka", [C, GB, L]), sb("kb", [C, GB, L]), sb("kk", [C, GB, L])
        kbd = sb("kbd", [C, GB, NH, L])
        vE = sb("vE", [L, GB, NH * HW + 2])
        nm2 = sb("nm2", [L, GB, NH])
        p2, pT2 = two("p2", [L, NH, L]), two("pT2", [L, NH, L])
        ri2, y = sb("ri2", [L, GB, NH]), two("y", [L, GB, C])
        yT, x2, sq = sb("yT", [C, GB, L]), sb("x2", [L, GB, C]), sb("sq", [L, C])
        ms, ve_t, r3 = sb("ms", [L, GB]), sb("ve_t", [L, GB]), sb("r3", [L, GB])
        fx = [two(f"fx{k}", [L, GB, ROW]) for k in range(2)]
        fT, bs = sb("fT", [C, GB, L]), two("bs", [L, GB, C])
        lg, mx8, ix8 = sb("lg", [L, GB, NE]), sb("mx8", [L, GB, 8]), sb("ix8", [L, GB, 8], U32)
        ixf, d8, e8 = sb("ixf", [L, 2, GB]), sb("d8", [L, GB, 8]), sb("e8", [L, GB, 8])
        se, s12, den, rden = sb("se", [L, GB]), sb("s12", [L, GB]), sb("den", [L, GB]), sb("rden", [L, GB])
        oh, ohb = sb("oh", [L, 2, GB, NE]), sb("ohb", [L, GB, NE], BF16)
        pos, mp = sb("pos", [L, GB, NE]), sb("mp", [L, 2, GB, NE])
        runc = two("runc", [128, NE])
        dcur = two("dcur", [L, 2 * GB])
        slotf = sb("slotf", [L, 2 * GB])
        slot = two("slot", [L, 2 * GB], I32)
        padx = sb("padx", [L, 2 * NE, ROW])
        cnt, cnti, nti = sb("cnt", [128, NE]), sb("cnti", [128, NE], I32), sb("nti", [128, NE], I32)
        ntf, jump, cum = sb("ntf", [128, NE]), sb("jump", [128, NE]), sb("cum", [128, NE])
        padi = sb("padi", [128, NE], I32)
        ex, tr, ty = two("ex", [1, NT]), two("tr", [1, NT]), sb("ty", [1, NT])
        exi, tri = sb("exi", [1, NT], I32), sb("tri", [1, NT], I32)
        xt = [sb(f"xt{i}", [128, ROW]) for i in range(4)]
        ys = [sb(f"ys{i}", [128, C]) for i in range(4)]
        xT, sg, hu, hsT = two("xT", [C, 128]), two("sg", [128, HID]), two("hu", [128, HID]), two("hsT", [128, 3, 128])
        c_in = [[x1[i], z[i], y[i]] for i in range(2)]
        c_s, c_o = [xs[0], xs[1]], [bs[0], bs[1]]

        bank = [ctx.enter_context(nc.psum_tensor(f"bank{i}", [128, 512], F32)) for i in range(8)]
        g0, g1, g2, g3, a0, a1, a3, t2 = bank
        gp = [g0, g1]
        h1_p, h3_p, x_p, hs_p, y_p = [g0, g1], [g2, g3], a0, a1, [a3, t2]

        names = """ld_c ld_w prep0 prep prep_ps half_ ready wscale xl0 xl1 al0 al1
        mask st_g mv_g ve_g rstd xn xnT_ps xnT hp_ps hE P_ps t u m1 e1 pT1_ps pT1 pv1 ri1 og x1
        st_a mv_a norm_a z hN hT_ps hT proj qa qb qT ka kb kk kd kp vE s_ps m2 e2
        pT2_ps pT2 pv2 ri2 y yT_ps yT wo_ps x2 sq ve_t r3 fx fT_ps fT lg_ps route e8 onehot
        rank_ps base bst0 bst1 sc0 sc1 padst padsc table
        tab xq0 xq1 xq2 xq3 xtr xT h1 h3 htr sg hu hsT yp ys zs0 zs1 zs2 zs3
        ci0 ci1 csum cnt_ cout ost0 ost1 turn_dve turn_pool""".split()
        S = {n: sem("s_" + n) for n in names}

        block = ctx.enter_context(nc.Block())

        def heads(ps, at, n):
            a = ps[:, 0:1]
            return bass.AP(a.tensor, a.offset + at, [a.ap[0], [128 + SKEW, NH], [1, n]])

        def late(v, k):
            return not isinstance(v, int) or v >= k

        def phase1(eng, body):
            body(0, 0, True, False, False)
            body(1, 1, True, True, False)
            body(2, 0, True, True, True)
            body(3, 1, True, True, True)
            with eng.Fori(2, NG // 2) as i:
                g = i * 2
                body(g, 0, True, True, True)
                body(g + 1, 1, True, True, True)
            body(NG, 0, False, True, True)
            body(NG + 1, 1, False, False, True)

        NCONST = 17 + 2 * NH

        @block.sync
        def _(sp):
            loads = [(ident[:], ident_h), (tmp_f[:, 0, :], causal_h), (tmp_f[:, 1, :], before_h),
                     (small[:], small_h), (tileno[:], tileno_h), (rope[:].rearrange("p a b -> p (a b)"), rope_h),
                     (ln1c[:], ln1.rearrange("(c a) -> c a", a=1)), (ln2c[:], ln2.rearrange("(c a) -> c a", a=1)),
                     (w_oc[:], W), (wv_s[:], wv), (wo_s[:], wo), (wh[:, :, 0:HD], WT.rearrange("c (h d) -> c h d", h=NH))]
            loads += [(projw[:, i, :], s) for i, s in enumerate((wq, wqr, wk, wkr))]
            for d, s in loads:
                sp.dma_start(d, s).then_inc(S["ld_c"], 16)
            sp.wait_ge(S["prep0"], 2)
            sp.dma_start(rout[:, 0:NE], router).then_inc(S["ld_c"], 16)
            for h in range(NH):
                sp.dma_start(att[h * HD:(h + 1) * HD, h:h + 1], att_src[h]).then_inc(S["ld_c"], 16)
                sp.dma_start(att[h * HD:(h + 1) * HD, NH + h:NH + h + 1], att_dst[h]).then_inc(S["ld_c"], 16)
            assert len(loads) + 1 + 2 * NH == NCONST

            def body(g, p, G, A, T):
                if G:
                    if late(g, 2):
                        sp.wait_ge(S["x1"], 4 * (g - 1))
                        sp.wait_ge(S["mask"], g - 1)
                    sp.dma_start(xs[p][:], x[bass.ds(g * GB, GB)].rearrange("b l c -> l b c")).then_inc(S[f"xl{p}"], 16)
                    sp.dma_start(adj8[p][:], adj[bass.ds(g * GB, GB)].rearrange("b l c -> l b c")).then_inc(S[f"al{p}"], 16)
                if isinstance(g, int) and g == 0:
                    sp.dma_start(w1_s[:], w1).then_inc(S["ld_w"], 16)
                    sp.dma_start(w3_s[:], w3).then_inc(S["ld_w"], 16)
                    for c, (o, n) in enumerate(HC):
                        sp.dma_start(w2_s[0:n, :, c, :], w2[:, o:o + n, :].rearrange("e p c -> p e c")).then_inc(S["ld_w"], 16)
                    sp.wait_ge(S["ready"], 2)
                    sp.dma_start(routed[NE * REGION * L:, :].rearrange("(i p) c -> p i c", p=L),
                                 padx[:, NE:2 * NE, :]).then_inc(S["padst"], 16)
                if T:
                    t = g - 2
                    sp.wait_ge(S["base"], t + 1)
                    sp.dma_start(base_d[bass.ds(t * GB * L, GB * L), :].rearrange("(b l) c -> l b c", l=L),
                                 bs[p][:]).then_inc(S[f"bst{p}"], 16)

            phase1(sp, body)

            sp.wait_ge(S["table"], 1)
            sp.wait_ge(S["padst"], 16)
            sp.wait_ge(S["sc0"], 8 * 16 * NG // 2)
            sp.wait_ge(S["sc1"], 8 * 16 * NG // 2)
            sp.wait_ge(S["padsc"], 16 * NE)
            by_tile = routed.rearrange("(n p) c -> n p c", p=L)

            def load_tile(k, r):
                tile = sp.value_load(tri[0:1, bass.ds(k + r, 1)], min_val=0, max_val=NE * REGION + NE - 1)
                if late(k, 4):
                    sp.wait_ge(S[f"zs{r}"], 4 * k)
                sp.dma_start(xt[r][:], by_tile[bass.ds(tile, 1)].rearrange("a p c -> p (a c)")).then_inc(S[f"xq{r}"], 16)

            for r in range(4):
                load_tile(0, r)
            with sp.Fori(1, NT // 4) as i:
                for r in range(4):
                    load_tile(i * 4, r)

            sp.wait_ge(S["bst0"], 16 * (NG // 2))
            sp.wait_ge(S["bst1"], 16 * (NG // 2))
            for r in range(4):
                sp.wait_ge(S[f"zs{r}"], 16 * NT // 4)
            srcs = [base_d.rearrange("(b l) c -> l b c", l=L)] + [
                parts[i * TOK:(i + 1) * TOK, :].rearrange("(b l) c -> l b c", l=L) for i in range(2)]

            def load_parts(g, p):
                if late(g, 2):
                    sp.wait_ge(S["cout"], g - 1)
                for d, s in zip(c_in[p], srcs):
                    sp.dma_start(d[:], s[:, bass.ds(g * GB, GB), :]).then_inc(S[f"ci{p}"], 16)

            load_parts(0, 0)
            load_parts(1, 1)
            with sp.Fori(1, NG // 2) as i:
                for p in range(2):
                    load_parts(i * 2 + p, p)

        @block.gpsimd
        def _(pool):
            pool.memset(att[:], 0.0).then_inc(S["prep0"], 1)
            pool.memset(rout[:], 0.0).then_inc(S["prep0"], 1)
            pool.memset(half[:], -0.5).then_inc(S["half_"], 1)
            pool.memset(hE[:], 1.0).then_inc(S["ready"], 0 + 1)
            pool.memset(padx[:], 0.0).then_inc(S["prep0"], 1)
            pool.wait_ge(S["prep0"], 3)
            pool.iota(padx[:, :, C].bitcast(I32), pattern=[[L, 2 * NE]], base=2 * TOK,
                      channel_multiplier=1).then_inc(S["ready"], 1)
            pool.memset(vE[:], 1.0).then_inc(S["ready"], 1)
            pool.memset(kbd[:], 0.0).then_inc(S["ready"], 1)
            pool.wait_ge(S["half_"], 1)
            pool.wait_ge(S["ready"], 4)

            def norm_step(ins, a, n):
                ins.then_inc(S["norm_a"], 1)
                pool.wait_ge(S["norm_a"], 7 * a + n)

            def body(g, p, G, A, T):
                a, t = g - 1, g - 2
                if G:
                    if late(g, 1):
                        pool.wait_ge(S["P_ps"], 4 * g)
                    pool.wait_ge(S[f"al{p}"], (g - p) * 8 + 16)
                    pool.sem_inc(S["turn_pool"], 1)
                    pool.tensor_scalar(mask[:], adj8[p][:], BIG, -BIG, ALU.mult, ALU.add).then_inc(S["mask"], 1)
                    pool.wait_ge(S["mv_g"], 4 * g + 4)
                    if late(g, 1):
                        pool.wait_ge(S["xn"], 4 * g)
                    pool.sem_inc(S["turn_pool"], 1)
                    pool.tensor_scalar(ve_g[:], mv_g[:, :, 1], EPS_LN, None, ALU.add).then_inc(S["ve_g"], 1)
                    pool.wait_ge(S["ve_g"], g + 1)
                    pool.tensor_tensor(rstd[:], ve_g[:], half[:], ALU.pow).then_inc(S["rstd"], 1)
                if A:
                    pool.wait_ge(S["mv_a"], 4 * a + 4)
                    if late(a, 1):
                        pool.wait_ge(S["hN"], 4 * a)
                    v = mv_a[:, :, 1]
                    pool.sem_inc(S["turn_pool"], 1)
                    norm_step(pool.tensor_scalar(va[:, 0, :], v, EPS_LN, None, ALU.add), a, 1)
                    norm_step(pool.tensor_tensor(r1[:], va[:, 0, :], half[:], ALU.pow), a, 2)
                    norm_step(pool.tensor_tensor(va[:, 1, :], v, r1[:], ALU.mult), a, 3)
                    norm_step(pool.tensor_tensor(va[:, 2, :], va[:, 1, :], r1[:], ALU.mult), a, 4)
                    pool.sem_inc(S["turn_pool"], 1)
                    norm_step(pool.tensor_scalar(va[:, 3, :], va[:, 2, :], EPS_RMS, None, ALU.add), a, 5)
                    norm_step(pool.tensor_tensor(r2[:], va[:, 3, :], half[:], ALU.pow), a, 6)
                    norm_step(pool.tensor_tensor(r12[:], r1[:], r2[:], ALU.mult), a, 7)
                if T:
                    pool.wait_ge(S["sq"], 4 * t + 4)
                    pool.sem_inc(S["turn_pool"], 1)
                    pool.tensor_scalar(ve_t[:], ms[:], 1.0 / C, EPS_RMS, ALU.mult, ALU.add).then_inc(S["ve_t"], 1)
                    if late(t, 1):
                        pool.wait_ge(S["fx"], 8 * t)
                    pool.wait_ge(S["ve_t"], t + 1)
                    pool.tensor_tensor(r3[:], ve_t[:], half[:], ALU.pow).then_inc(S["r3"], 1)
                def add_x1(j):
                    pool.wait_ge(S["og"], 4 * g + j + 1)
                    if j == 0 and late(g, 2):
                        pool.wait_ge(S["hN"], 4 * (g - 1))
                        pool.wait_ge(S["base"], g - 1)
                    pool.tensor_tensor(x1[p][:, j, :], xs[p][:, j, :], og[:, j, :], ALU.add).then_inc(S["x1"], 1)

                if T:
                    pool.wait_ge(S["x2"], t + 1)
                    if late(t, 2):
                        pool.wait_ge(S[f"bst{p}"], 8 * (t - p))
                    pool.tensor_tensor(bs[p][:], x1[p][:], x2[:], ALU.add).then_inc(S["base"], 1)
                if G:
                    add_x1(0)
                    add_x1(1)
                if T:
                    pool.wait_ge(S["route"], ROUTE * t + ROUTE)
                    pool.sem_inc(S["turn_pool"], 1)
                    for k in range(2):
                        for j in range(GB):
                            i = k * GB + j
                            pool.indirect_dma_start(routed, bass.IndirectOffsetOnAxis(slot[p][:, i:i + 1], 0),
                                                    fx[k][p][:, j, :], None).then_inc(S[f"sc{p}"], 16)
                if G:
                    add_x1(2)
                    add_x1(3)

            phase1(pool, body)
            pool.wait_ge(S["tab"], 1)
            for e in range(NE):
                pool.indirect_dma_start(routed, bass.IndirectOffsetOnAxis(padi[:, e:e + 1], 0),
                                        padx[:, e, :], None).then_inc(S["padsc"], 16)
            with pool.Fori(0, NT // 4) as i:
                k = i * 4
                for r in range(4):
                    pool.wait_ge(S["ys"], k + r + 1)
                    pool.sem_inc(S["turn_pool"], 1)
                    pool.indirect_dma_start(parts, bass.IndirectOffsetOnAxis(xt[r][:, C:C + 1].bitcast(I32), 0),
                                            ys[r][:], None).then_inc(S[f"zs{r}"], 16)

        @block.scalar
        def _(act):
            def body(g, p, G, A, T):
                a, t = g - 1, g - 2
                if T:
                    act.wait_ge(S["yT_ps"], t + 1)
                    if late(t, 1):
                        act.wait_ge(S["wo_ps"], t)
                    act.activation(yT[:].rearrange("c b l -> c (b l)"), t2[:], ACT.Copy).then_inc(S["yT"], 1)
                if G:
                    act.wait_ge(S["xnT_ps"], g + 1)
                    if late(g, 1):
                        act.wait_ge(S["P_ps"], 4 * g)
                    act.activation(xnT[:].rearrange("c b l -> c (b l)"), g3[:], ACT.Copy).then_inc(S["xnT"], 1)
                if A:
                    act.wait_ge(S["hT_ps"], a + 1)
                    if late(a, 1):
                        act.wait_ge(S["proj"], 5 * a)
                    act.activation(hT[:].rearrange("c b l -> c (b l)"), a3[:], ACT.Copy).then_inc(S["hT"], 1)
                if G:
                    act.wait_ge(S["hp_ps"], g + 1)
                    if late(g, 1):
                        act.wait_ge(S["pv1"], 4 * g)
                        act.wait_ge(S["t"], 4 * g)
                    for i in range(2):
                        act.activation(hE[:, 2 * i:2 * i + 2, 0:NH * GW].rearrange("p b (h w) -> p b h w", w=GW)[:, :, :, 0:HD + 1],
                                       gp[i][:, 0:2 * NH * (HD + 1)].rearrange("p (b h w) -> p b h w", b=2, h=NH),
                                       ACT.Copy).then_inc(S["hE"], 1)
                if A:
                    act.wait_ge(S["proj"], 5 * a + 5)
                    if late(a, 1):
                        act.wait_ge(S["pv2"], 4 * a)
                    act.activation(vE[:, :, 0:NH * HW].rearrange("p b (h w) -> p b h w", w=HW)[:, :, :, 0:HD],
                                   a1[:].rearrange("p (b h w) -> p b h w", b=GB, h=NH), ACT.Copy).then_inc(S["vE"], 1)
                if A:
                    act.wait_ge(S["kk"], a + 1)
                    if late(a, 1):
                        act.wait_ge(S["s_ps"], 4 * a)
                    for h in (2, 3):
                        o = slice(h * HD, (h + 1) * HD)
                        act.activation(kbd[o, :, h, :], kk[o, :, :], ACT.Copy).then_inc(S["kp"], 1)
                if T:
                    act.wait_ge(S["fT_ps"], t + 1)
                    if late(t, 1):
                        act.wait_ge(S["lg_ps"], t)
                    act.activation(fT[:].rearrange("c b l -> c (b l)"), t2[:], ACT.Copy).then_inc(S["fT"], 1)

                def exp1(j):
                    act.wait_ge(S["m1"], 4 * g + j + 1)
                    if late(g, 1) or j >= 2:
                        act.wait_ge(S["pT1_ps"], 4 * g + j - 1)
                    for h in range(NH):
                        last = act.activation(p1[j % 2][:, h, :], ub[j % 2][:, h, :], ACT.Exp, bias=nm1[:, j, h:h + 1])
                    last.then_inc(S["e1"], 1)

                def exp2(j):
                    act.wait_ge(S["m2"], 4 * a + j + 1)
                    if late(a, 1) or j >= 2:
                        act.wait_ge(S["pT2_ps"], 4 * a + j - 1)
                    for h in range(NH):
                        last = act.activation(p2[j % 2][:, h, :], a0[:, h * L:(h + 1) * L], ACT.Exp, bias=nm2[:, j, h:h + 1])
                    last.then_inc(S["e2"], 1)

                def out1(j):
                    act.wait_ge(S["pT1_ps"], 4 * g + j + 1)
                    if late(g, 1) or j >= 2:
                        act.wait_ge(S["pv1"], 4 * g + j - 1)
                    act.activation(pT1[j % 2][:].rearrange("c b l -> c (b l)"), g2[:], ACT.Copy).then_inc(S["pT1"], 1)

                def out2(j):
                    act.wait_ge(S["pT2_ps"], 4 * a + j + 1)
                    if late(a, 1) or j >= 2:
                        act.wait_ge(S["pv2"], 4 * a + j - 1)
                    act.activation(pT2[j % 2][:].rearrange("c b l -> c (b l)"), a1[:], ACT.Copy).then_inc(S["pT2"], 1)

                if G:
                    exp1(0)
                if T:
                    act.wait_ge(S["route"], ROUTE * t + 10)
                    act.activation(e8[:], d8[:], ACT.Exp).then_inc(S["e8"], 1)
                if A:
                    exp2(0)
                for j in range(1, GB + 1):
                    if G and j < GB:
                        exp1(j)
                    if G:
                        out1(j - 1)
                    if A:
                        out2(j - 1)
                    if A and j < GB:
                        exp2(j)
                if isinstance(g, int) and g == 1:
                    act.wait_ge(S["ld_w"], 16 * 5)
                    act.activation(w1_s[:], w1_s[:], ACT.Copy, scale=ln2c[:]).then_inc(S["wscale"], 1)
                    act.activation(w3_s[:], w3_s[:], ACT.Copy, scale=ln2c[:]).then_inc(S["wscale"], 1)

            act.wait_ge(S["ready"], 4)
            act.wait_ge(S["prep"], 1)
            phase1(act, body)

            def gate(k, q):
                act.wait_ge(S["h1"], k + 1)
                if late(k, 2):
                    act.wait_ge(S["hu"], k - 1)
                act.activation(sg[q][:], h1_p[q][:, 0:HID], ACT.Silu).then_inc(S["sg"], 1)

            def out_h(k, q):
                act.wait_ge(S["htr"], k + 1)
                if late(k, 2):
                    act.wait_ge(S["yp"], k - 1)
                act.activation(hsT[q][:, 0:2, :].rearrange("p a b -> p (a b)"), hs_p[:, 0:256], ACT.Copy)
                act.activation(hsT[q][0:HC[2][1], 2, :], hs_p[0:HC[2][1], 256:384], ACT.Copy).then_inc(S["hsT"], 1)

            gate(0, 0)
            gate(1, 1)
            out_h(0, 0)
            with act.Fori(1, NT // 2) as i:
                k = i * 2
                for q in range(2):
                    gate(k + q, q)
                    out_h(k + q - 1, 1 - q)
            out_h(NT - 1, 1)

            with act.Fori(0, NG // 2) as i:
                g = i * 2
                for p in range(2):
                    act.wait_ge(S["cout"], g + p + 1)
                    act.dma_start(out[bass.ds((g + p) * GB, GB)].rearrange("b l c -> l b c"), c_o[p][:]).then_inc(S[f"ost{p}"], 16)
            act.wait_ge(S["ost0"], 16 * (NG // 2))
            act.wait_ge(S["ost1"], 16 * (NG // 2))

        @block.vector
        def _(dve):
            dve.wait_ge(S["ld_c"], 16 * NCONST)
            dve.wait_ge(S["prep0"], 2)
            dve.memset(onesb[:], 1.0)
            dve.tensor_copy(identb[:], ident[:])
            dve.tensor_copy(causal[:], tmp_f[:, 0, :])
            dve.tensor_copy(before[:], tmp_f[:, 1, :])
            dve.tensor_copy(runc[1][:], region0)
            dve.tensor_copy(dcur[1][:], small[:, 3 * NE + 1:])
            dve.tensor_scalar(projw[:], projw[:], ln1c[:], None, ALU.mult)
            dve.tensor_scalar(wv_s[:], wv_s[:], ln1c[:], None, ALU.mult)
            dve.tensor_scalar(rout[:], rout[:], ln2c[:], None, ALU.mult)
            dve.wait_ge(S["prep_ps"], 1)
            dve.tensor_copy(wh[:, :, HD], a0[:, 0:NH])
            dve.tensor_copy(wd[:], a0[:, NH:2 * NH].unsqueeze(2).broadcast_to([C, NH, L])).then_inc(S["prep"], 1)
            dve.wait_ge(S["prep"], 1)
            dve.wait_ge(S["ready"], 4)

            def body(g, p, G, A, T):
                a, t, pa = g - 1, g - 2, 1 - p
                n_route = [0]

                def link(ins, last=True):
                    n_route[0] += 1
                    ins.then_inc(S["route"], 1)
                    if last:
                        dve.wait_ge(S["route"], ROUTE * t + n_route[0])

                if G:
                    dve.wait_ge(S[f"xl{p}"], (g - p) * 8 + 16)
                    if late(g, 1):
                        dve.wait_ge(S["ve_g"], g)
                        dve.wait_ge(S["xn"], 4 * g)
                    for j in range(GB):
                        dve.bn_stats(st_g[:, j, :], xs[p][:, j, :]).then_inc(S["st_g"], 1)
                    for j in range(GB):
                        dve.wait_ge(S["st_g"], 4 * g + j + 1)
                        dve.sem_inc(S["turn_dve"], 1)
                        dve.bn_aggr(mv_g[:, j, :], st_g[:, j, :]).then_inc(S["mv_g"], 1)
                if A:
                    dve.wait_ge(S["x1"], 4 * a + 4)
                    if late(a, 1):
                        dve.wait_ge(S["norm_a"], 7 * a)
                        dve.wait_ge(S["hN"], 4 * a)
                    for j in range(GB):
                        dve.bn_stats(st_a[:, j, :], x1[pa][:, j, :]).then_inc(S["st_a"], 1)
                    for j in range(GB):
                        dve.wait_ge(S["st_a"], 4 * a + j + 1)
                        dve.sem_inc(S["turn_dve"], 1)
                        dve.bn_aggr(mv_a[:, j, :], st_a[:, j, :]).then_inc(S["mv_a"], 1)
                if G:
                    dve.wait_ge(S["rstd"], g + 1)
                    if late(g, 1):
                        dve.wait_ge(S["xnT_ps"], g)
                    for j in range(GB):
                        dve.tensor_scalar(xn[:, j, :], xs[p][:, j, :], mv_g[:, j, 0:1], rstd[:, j:j + 1],
                                          ALU.subtract, ALU.mult).then_inc(S["xn"], 1)
                if A:
                    dve.wait_ge(S["norm_a"], 7 * a + 7)
                    if late(a, 1):
                        dve.wait_ge(S["hT_ps"], a)
                    if late(a, 2):
                        dve.wait_ge(S["x2"], a - 1)
                    for j in range(GB):
                        dve.tensor_scalar(hN[:, j, :], x1[pa][:, j, :], mv_a[:, j, 0:1], r12[:, j:j + 1],
                                          ALU.subtract, ALU.mult)
                        dve.tensor_scalar(z[pa][:, j, :], x1[pa][:, j, :], mv_a[:, j, 0:1], r1[:, j:j + 1],
                                          ALU.subtract, ALU.mult).then_inc(S["hN"], 1)
                if T:
                    dve.wait_ge(S["wo_ps"], t + 1)
                    if late(t, 1):
                        dve.wait_ge(S["base"], t)
                        dve.wait_ge(S["fx"], 8 * t)
                        dve.wait_ge(S["ve_t"], t)
                    dve.tensor_tensor(x2[:].rearrange("p b c -> p (b c)"), t2[:],
                                      z[p][:].rearrange("p b c -> p (b c)"), ALU.add).then_inc(S["x2"], 1)
                    dve.wait_ge(S["x2"], t + 1)
                    for j in range(GB):
                        if j or late(t, 1):
                            dve.wait_ge(S["sq"], 4 * t + j)
                        dve.tensor_tensor_reduce(out=sq[:], in0=x2[:, j, :], in1=x2[:, j, :], scale=1.0, scalar=0.0,
                                                 op0=ALU.mult, op1=ALU.add, accum_out=ms[:, j:j + 1]).then_inc(S["sq"], 1)
                if T:
                    dve.wait_ge(S["r3"], t + 1)
                    if late(t, 2):
                        dve.wait_ge(S[f"sc{p}"], 64 * (t - p))
                    for j in range(GB):
                        for k in range(2):
                            dve.tensor_scalar(fx[k][p][:, j, 0:C], x2[:, j, :], r3[:, j:j + 1], None,
                                              ALU.mult).then_inc(S["fx"], 1)
                if A:
                    def turn(dst, src, i, n):
                        dve.wait_ge(S["proj"], 5 * a + n)
                        return dve.tensor_tensor(dst[:], src[:].rearrange("c (b l) -> c b l", b=GB),
                                                 rope[:, i, :].unsqueeze(1).broadcast_to([C, GB, L]), ALU.mult)

                    if late(a, 1):
                        dve.wait_ge(S["s_ps"], 4 * a)
                        dve.wait_ge(S["kp"], 2 * a)
                        dve.wait_ge(S["kd"], 2 * a)
                    turn(qa, a0, 0, 1).then_inc(S["qa"], 1)
                    turn(qb, a1, 1, 2).then_inc(S["qb"], 1)
                    dve.wait_ge(S["qa"], a + 1)
                    dve.wait_ge(S["qb"], a + 1)
                    dve.tensor_tensor(qT[:], qa[:], qb[:], ALU.add).then_inc(S["qT"], 1)
                    turn(ka, a3, 2, 3).then_inc(S["ka"], 1)
                    turn(kb, a0, 3, 4).then_inc(S["kb"], 1)
                    dve.wait_ge(S["ka"], a + 1)
                    dve.wait_ge(S["kb"], a + 1)
                    dve.tensor_tensor(kk[:], ka[:], kb[:], ALU.add).then_inc(S["kk"], 1)
                    dve.wait_ge(S["kk"], a + 1)
                    for h in (0, 1):
                        o = slice(h * HD, (h + 1) * HD)
                        dve.tensor_copy(kbd[o, :, h, :], kk[o, :, :]).then_inc(S["kd"], 1)

                def scores1(j):
                    dve.wait_ge(S["P_ps"], 4 * g + j + 1)
                    dve.wait_ge(S["hE"], 2 * g + 2)
                    if late(g, 1) or j:
                        dve.wait_ge(S["u"], 4 * g + j)
                    dve.tensor_tensor(tb[:], gp[j % 2][:].rearrange("p (h l) -> p h l", h=NH),
                                      hE[:, j, 0:NH * GW].rearrange("p (h w) -> p h w", w=GW)[:, :, HD:HD + 1].broadcast_to([L, NH, L]),
                                      ALU.add).then_inc(S["t"], 1)
                    dve.wait_ge(S["t"], 4 * g + j + 1)
                    if late(g, 1) or j >= 2:
                        dve.wait_ge(S["e1"], 4 * g + j - 1)
                    u = ub[j % 2]
                    dve.scalar_tensor_tensor(out=u[:].rearrange("p h l -> p (h l)"), in0=tb[:].rearrange("p h l -> p (h l)"), scalar=0.2,
                                             in1=tb[:].rearrange("p h l -> p (h l)"), op0=ALU.mult, op1=ALU.max).then_inc(S["u"], 1)
                    dve.wait_ge(S["u"], 4 * g + j + 1)
                    if late(g, 1) and j == 0:
                        dve.wait_ge(S["e1"], 4 * g)
                    dve.tensor_reduce(nm1[:, j, :], u[:], AX.X, ALU.max, negate=True).then_inc(S["m1"], 1)

                def max2(j):
                    dve.wait_ge(S["s_ps"], 4 * a + j + 1)
                    if late(a, 1) and j == 0:
                        dve.wait_ge(S["e2"], 4 * a)
                    dve.tensor_reduce(nm2[:, j, :], a0[:].rearrange("p (h l) -> p h l", h=NH), AX.X, ALU.max,
                                      negate=True).then_inc(S["m2"], 1)

                def mix(j, ps, pv, ri, s_ri, dst, s_dst, one, n):
                    dve.wait_ge(S[pv], 4 * n + j + 1)
                    dve.reciprocal(ri[:, j, :], heads(ps, one, 1).rearrange("p h a -> p (h a)")).then_inc(S[s_ri], 1)
                    dve.wait_ge(S[s_ri], 4 * n + j + 1)
                    dve.tensor_tensor(dst[:, j, :].rearrange("p (h d) -> p h d", h=NH), heads(ps, 0, HD),
                                      ri[:, j, :].unsqueeze(2).broadcast_to([L, NH, HD]), ALU.mult).then_inc(S[s_dst], 1)

                def mix1(j):
                    if late(g, 1) and j == 0:
                        dve.wait_ge(S["x1"], 4 * g)
                    mix(j, g3, "pv1", ri1, "ri1", og, "og", GW - 1, g)

                def mix2(j):
                    if late(a, 2) and j == 0:
                        dve.wait_ge(S["yT_ps"], a - 1)
                    mix(j, a3, "pv2", ri2, "ri2", y[pa], "y", HD, a)

                def route1():
                    dve.wait_ge(S["lg_ps"], t + 1)
                    link(dve.tensor_copy(lg[:], t2[:].rearrange("p (b n) -> p b n", b=GB)[:, :, 0:NE]))
                    dve.sem_inc(S["turn_dve"], 1)
                    for j in range(GB):
                        link(dve.max(mx8[:, j, :], lg[:, j, :]), j == GB - 1)
                    dve.sem_inc(S["turn_dve"], 1)
                    for j in range(GB):
                        link(dve.max_index(ix8[:, j, :], mx8[:, j, :], lg[:, j, :]), j == GB - 1)
                    if late(t, 1):
                        dve.wait_ge(S["e8"], t)
                    link(dve.tensor_tensor(d8[:], mx8[:], mx8[:, :, 0:1].broadcast_to([L, GB, 8]), ALU.subtract), False)
                    link(dve.tensor_copy(ixf[:].rearrange("p k b -> p b k"), ix8[:, :, 0:2]))
                    n8 = 2 * GB
                    link(dve.tensor_tensor(oh[:].rearrange("p k b e -> p (k b) e"), expno.unsqueeze(1).broadcast_to([L, n8, NE]),
                                           ixf[:].rearrange("p k b -> p (k b)").unsqueeze(2).broadcast_to([L, n8, NE]), ALU.is_equal))
                    if late(t, 1):
                        dve.wait_ge(S["rank_ps"], t)
                    link(dve.tensor_tensor(ohb[:], oh[:, 0], oh[:, 1], ALU.add), False)
                    dve.wait_ge(S["e8"], t + 1)
                    link(dve.tensor_reduce(se[:], e8[:], AX.X, ALU.add), False)
                    link(dve.tensor_tensor(s12[:], e8[:, :, 0], e8[:, :, 1], ALU.add))
                    link(dve.scalar_tensor_tensor(out=den[:], in0=se[:], scalar=EPS_TOP, in1=s12[:], op0=ALU.mult, op1=ALU.add))
                    link(dve.reciprocal(rden[:], den[:]))
                    for k in range(2):
                        link(dve.tensor_tensor(fx[k][p][:, :, C + 1], e8[:, :, k], rden[:], ALU.mult), k == 1)
                    link(dve.tensor_scalar(dcur[p][:], dcur[1 - p][:], float(GB * L), None, ALU.add))
                    for k in range(2):
                        link(dve.tensor_copy(fx[k][p][:, :, C].bitcast(I32), dcur[p][:, k * GB:(k + 1) * GB]), k == 1)

                def route2():
                    dve.wait_ge(S["rank_ps"], t + 1)
                    link(dve.tensor_tensor(pos[:], t2[:, 0:GB * NE].rearrange("p (b e) -> p b e", e=NE),
                                           runc[1 - p][:].unsqueeze(1).broadcast_to([L, GB, NE]), ALU.add), False)
                    link(dve.tensor_tensor(runc[p][:], t2[:, GB * NE:(GB + 1) * NE], runc[1 - p][:], ALU.add))
                    for k in range(2):
                        link(dve.tensor_tensor(mp[:, k], oh[:, k], pos[:], ALU.mult), k == 1)
                    link(dve.tensor_reduce(slotf[:], mp[:].rearrange("p k b e -> p (k b) e"), AX.X, ALU.add))
                    link(dve.tensor_copy(slot[p][:], slotf[:]))

                if G:
                    scores1(0)
                if T:
                    route1()
                if A:
                    max2(0)
                if G:
                    scores1(1)
                if T:
                    route2()
                for j in range(GB):
                    if A and j + 1 < GB:
                        max2(j + 1)
                    if G:
                        mix1(j)
                    if A:
                        mix2(j)
                    if G and j + 2 < GB:
                        scores1(j + 2)
                assert n_route[0] in (0, ROUTE)

            phase1(dve, body)

            steps = [0]

            def link(ins):
                steps[0] += 1
                ins.then_inc(S["csum"], 1)
                dve.wait_ge(S["csum"], steps[0])

            end = runc[(NG - 1) % 2]
            link(dve.tensor_scalar(padi[:], end[:], partno, None, ALU.add))
            dve.nop().then_inc(S["tab"], 1)
            link(dve.tensor_tensor(cnt[:], end[:], region0, ALU.subtract))
            link(dve.tensor_scalar(cnti[:], cnt[:], float(L - 1), None, ALU.add))
            link(dve.tensor_scalar(nti[:], cnti[:], 7, None, ALU.arith_shift_right))
            link(dve.tensor_copy(ntf[:], nti[:]))
            link(dve.tensor_scalar(jump[:], ntf[:], -1.0, float(REGION), ALU.mult, ALU.add))
            link(dve.tensor_copy(cum[:, 0:1], ntf[:, 0:1]))
            for e in range(1, NE):
                link(dve.tensor_tensor(cum[:, e:e + 1], cum[:, e - 1:e], ntf[:, e:e + 1], ALU.add))
            link(dve.memset(ex[0][:], 0.0))
            link(dve.tensor_copy(tr[0][:], tileno[:]))
            for e in range(NE):
                i, o = e % 2, 1 - e % 2
                link(dve.scalar_tensor_tensor(out=ex[o][:], in0=tileno[:], scalar=cum[0:1, e:e + 1], in1=ex[i][:],
                                              op0=ALU.is_ge, op1=ALU.add))
                link(dve.tensor_scalar(ty[:], tileno[:], cum[0:1, e:e + 1], jump[0:1, e:e + 1], ALU.is_ge, ALU.mult))
                link(dve.tensor_tensor(tr[o][:], tr[i][:], ty[:], ALU.add))
            link(dve.tensor_scalar(exi[:], ex[0][:], float(NE - 1), None, ALU.min))
            link(dve.tensor_copy(tri[:], tr[0][:]))
            dve.nop().then_inc(S["table"], 1)

            def out_x(k, q):
                dve.wait_ge(S["xtr"], k + 1)
                if late(k, 2):
                    dve.wait_ge(S["h3"], k - 1)
                dve.tensor_copy(xT[q][:], x_p[:, 0:128]).then_inc(S["xT"], 1)

            def gated(k, q):
                dve.wait_ge(S["h3"], k + 1)
                dve.wait_ge(S["sg"], k + 1)
                if late(k, 2):
                    dve.wait_ge(S["htr"], k - 1)
                dve.tensor_tensor(hu[q][:], h3_p[q][:, 0:HID], sg[q][:], ALU.mult).then_inc(S["hu"], 1)

            def weigh(k, r):
                dve.wait_ge(S["yp"], k + 1)
                if late(k, 4):
                    dve.wait_ge(S[f"zs{r}"], 4 * (k - r))
                dve.tensor_scalar(ys[r][:], y_p[r % 2][:, 0:C], xt[r][:, C + 1:C + 2], None, ALU.mult).then_inc(S["ys"], 1)

            def step(k, r, first, last):
                if not last:
                    out_x(k + 1, (r + 1) % 2)
                gated(k, r % 2)
                if not first:
                    weigh(k - 1, (r - 1) % 4)

            out_x(0, 0)
            for k in range(8):
                step(k, k % 4, k == 0, False)
            with dve.Fori(2, NT // 4 - 1) as i:
                k = i * 4
                for r in range(4):
                    step(k + r, r, False, False)
            for r in range(4):
                step(NT - 4 + r, r, False, r == 3)
            weigh(NT - 1, 3)

            def total(g, p):
                dve.wait_ge(S[f"ci{p}"], 24 * (g - p) + 48)
                b_, y0, y1 = c_in[p]
                if late(g, 2):
                    dve.wait_ge(S[f"ost{p}"], 8 * (g - p))
                dve.tensor_tensor(c_s[p][:], y0[:], y1[:], ALU.add).then_inc(S["cnt_"], 1)
                dve.wait_ge(S["cnt_"], g + 1)
                dve.tensor_tensor(c_o[p][:], c_s[p][:], b_[:], ALU.add).then_inc(S["cout"], 1)

            total(0, 0)
            total(1, 1)
            with dve.Fori(1, NG // 2) as i:
                for p in range(2):
                    total(i * 2 + p, p)

        @block.tensor
        def _(pe):
            pe.wait_ge(S["ld_c"], 16 * NCONST)
            pe.matmul(a0[:, 0:2 * NH], w_oc[:], att[:], start=True, stop=True).then_inc(S["prep_ps"], 1)
            pe.wait_ge(S["prep"], 1)
            pe.wait_ge(S["ready"], 4)

            def flip(ps, src, n=GB):
                for j in range(n):
                    last = pe.transpose(ps[:, j * 128:(j + 1) * 128], src[:, j, 0:128], ident[:])
                return last

            def body(g, p, G, A, T):
                a, t, pa = g - 1, g - 2, 1 - p
                if T:
                    pe.wait_ge(S["y"], 4 * t + 4)
                    if late(t, 1):
                        pe.wait_ge(S["route"], ROUTE * t)
                    flip(t2, y[p]).then_inc(S["yT_ps"], 1)
                if G:
                    pe.wait_ge(S["xn"], 4 * g + 4)
                    if late(g, 1):
                        pe.wait_ge(S["og"], 4 * g)
                    flip(g3, xn).then_inc(S["xnT_ps"], 1)
                if A:
                    pe.wait_ge(S["hN"], 4 * a + 4)
                    if late(a, 1):
                        pe.wait_ge(S["y"], 4 * a)
                    flip(a3, hN).then_inc(S["hT_ps"], 1)
                if T:
                    pe.wait_ge(S["yT"], t + 1)
                    for j in range(GB):
                        last = pe.matmul(t2[:, j * C:(j + 1) * C], yT[:, j, :], wo_s[:], start=True, stop=True)
                    last.then_inc(S["wo_ps"], 1)
                if G:
                    pe.wait_ge(S["xnT"], g + 1)
                    if late(g, 1):
                        pe.wait_ge(S["t"], 4 * g)
                    w = NH * (HD + 1)
                    for j in range(GB):
                        last = pe.matmul(gp[j // 2][:, (j % 2) * w:(j % 2 + 1) * w], xnT[:, j, :],
                                         wh[:].rearrange("c h w -> c (h w)"), start=True, stop=True)
                    last.then_inc(S["hp_ps"], 1)
                if A:
                    pe.wait_ge(S["hT"], a + 1)
                    if late(a, 1):
                        pe.wait_ge(S["e2"], 4 * a)
                        pe.wait_ge(S["pT2"], 4 * a)
                    hTf = hT[:].rearrange("c b l -> c (b l)")
                    pe.matmul(a0[:], projw[:, 0, :], hTf, start=True, stop=True).then_inc(S["proj"], 1)
                    pe.matmul(a1[:], projw[:, 1, :], hTf, start=True, stop=True).then_inc(S["proj"], 1)
                    pe.matmul(a3[:], projw[:, 2, :], hTf, start=True, stop=True).then_inc(S["proj"], 1)
                    pe.wait_ge(S["qa"], a + 1)
                    pe.matmul(a0[:], projw[:, 3, :], hTf, start=True, stop=True).then_inc(S["proj"], 1)
                    pe.wait_ge(S["qb"], a + 1)
                    for j in range(GB):
                        last = pe.matmul(a1[:, j * C:(j + 1) * C], hT[:, j, :], wv_s[:], start=True, stop=True)
                    last.then_inc(S["proj"], 1)

                def term1(j):
                    pe.wait_ge(S["mask"], g + 1)
                    if j < 2:
                        pe.wait_ge(S["hE"], 2 * g + 2)
                    else:
                        pe.wait_ge(S["t"], 4 * g + j - 1)
                    ps = gp[j % 2]
                    pe.matmul(ps[:].rearrange("p (h l) -> p h l", h=NH), identb[:],
                              mask[:, j, :].unsqueeze(1).broadcast_to([L, NH, L]), start=True, stop=False)
                    for h in range(NH):
                        last = pe.matmul(ps[:, h * L:(h + 1) * L], wd[:, h, :], xnT[:, j, :], start=False, stop=h == NH - 1)
                    last.then_inc(S["P_ps"], 1)

                def score2(j):
                    if j == 0:
                        pe.wait_ge(S["qT"], a + 1)
                        pe.wait_ge(S["kd"], 2 * a + 2)
                        pe.wait_ge(S["kp"], 2 * a + 2)
                    else:
                        pe.wait_ge(S["e2"], 4 * a + j)
                    pe.matmul(a0[:].rearrange("p (h l) -> p h l", h=NH), identb[:],
                              causal[:].unsqueeze(1).broadcast_to([L, NH, L]), start=True, stop=False)
                    pe.matmul(a0[:], qT[:, j, :], kbd[:, j].rearrange("c h l -> c (h l)"), start=False, stop=True).then_inc(S["s_ps"], 1)

                def probs1(j):
                    pe.wait_ge(S["e1"], 4 * g + j + 1)
                    if late(g, 1) or j:
                        pe.wait_ge(S["pT1"], 4 * g + j)
                    flip(g2, p1[j % 2]).then_inc(S["pT1_ps"], 1)

                def probs2(j):
                    pe.wait_ge(S["e2"], 4 * a + j + 1)
                    if j:
                        pe.wait_ge(S["pT2"], 4 * a + j)
                    else:
                        pe.wait_ge(S["vE"], a + 1)
                    flip(a1, p2[j % 2]).then_inc(S["pT2_ps"], 1)

                def values1(j):
                    pe.wait_ge(S["pT1"], 4 * g + j + 1)
                    if j:
                        pe.wait_ge(S["og"], 4 * g + j)
                    for h in range(NH):
                        o = h * (GW - SKEW)
                        last = pe.matmul(g3[:, h * 128:(h + 1) * 128], pT1[j % 2][:, h, :], hE[:, j, o:o + 128], start=True, stop=True)
                    last.then_inc(S["pv1"], 1)

                def values2(j):
                    pe.wait_ge(S["pT2"], 4 * a + j + 1)
                    if j:
                        pe.wait_ge(S["y"], 4 * a + j)
                    else:
                        pe.wait_ge(S["ka"], a + 1)
                    for h in range(NH):
                        o = h * (HW - SKEW)
                        last = pe.matmul(a3[:, h * 128:(h + 1) * 128], pT2[j % 2][:, h, :], vE[:, j, o:o + 128], start=True, stop=True)
                    last.then_inc(S["pv2"], 1)

                if T:
                    pe.wait_ge(S["fx"], 8 * t + 8)
                    flip(t2, fx[0][p]).then_inc(S["fT_ps"], 1)
                if G:
                    term1(0)
                if T:
                    pe.wait_ge(S["fT"], t + 1)
                    for j in range(GB):
                        last = pe.matmul(t2[:, j * 128:(j + 1) * 128], fT[:, j, :], rout[:], start=True, stop=True)
                    last.then_inc(S["lg_ps"], 1)
                if G:
                    term1(1)
                if A:
                    score2(0)
                if T:
                    pe.wait_ge(S["route"], ROUTE * t + 13)
                    for j in range(GB + 1):
                        o = t2[:, j * NE:(j + 1) * NE]
                        if j < GB:
                            last = pe.matmul(o, before[:], ohb[:, j, :], start=True, stop=j == 0)
                        for i in range(j):
                            last = pe.matmul(o, onesb[:], ohb[:, i, :], start=j == GB and i == 0, stop=i == j - 1)
                    last.then_inc(S["rank_ps"], 1)
                for j in range(GB):
                    if G:
                        probs1(j)
                    if A:
                        probs2(j)
                    if A and j + 1 < GB:
                        score2(j + 1)
                    if G:
                        values1(j)
                    if A:
                        values2(j)
                    if G and j + 2 < GB:
                        term1(j + 2)

            phase1(pe, body)

            pe.wait_ge(S["wscale"], 2)
            pe.wait_ge(S["table"], 1)

            def turn_x(k, r):
                pe.wait_ge(S[f"xq{r}"], 4 * (k - r) + 16)
                if late(k, 1):
                    pe.wait_ge(S["xT"], k)
                pe.transpose(x_p[:, 0:128], xt[r][:, 0:C], ident[:]).then_inc(S["xtr"], 1)

            def up(w, ps, k, q, e, s, used):
                if late(k, 2):
                    pe.wait_ge(S[used], k - 1)
                pe.matmul(ps[q][:, 0:HID], xT[q][:], w[:, bass.ds(e, 1), :].rearrange("c a n -> c (a n)"),
                          start=True, stop=True).then_inc(S[s], 1)

            def turn_h(k, q):
                pe.wait_ge(S["hu"], k + 1)
                if late(k, 1):
                    pe.wait_ge(S["hsT"], k)
                for c, (o, n) in enumerate(HC):
                    last = pe.transpose(hs_p[0:n, c * 128:(c + 1) * 128], hu[q][:, o:o + n], ident[:])
                last.then_inc(S["htr"], 1)

            def down(k, q, e):
                pe.wait_ge(S["hsT"], k + 1)
                if late(k, 2):
                    pe.wait_ge(S["ys"], k - 1)
                for c, (o, n) in enumerate(HC):
                    last = pe.matmul(y_p[q][:, 0:C], hsT[q][0:n, c, :], w2_s[0:n, bass.ds(e, 1), c, :].rearrange("p a c -> p (a c)"),
                                     start=c == 0, stop=c == 2)
                last.then_inc(S["yp"], 1)

            def expert(k):
                return pe.value_load(exi[0:1, bass.ds(k, 1)], min_val=0, max_val=NE - 1)

            def step(k, r, first, last):
                e = expert(k)
                q = r % 2
                if not last:
                    turn_x(k + 1, (r + 1) % 4)
                pe.wait_ge(S["xT"], k + 1)
                up(w1_s, h1_p, k, q, e, "h1", "sg")
                if not first:
                    turn_h(k - 1, 1 - q)
                up(w3_s, h3_p, k, q, e, "h3", "hu")
                if not first:
                    down(k - 1, 1 - q, expert(k - 1))

            turn_x(0, 0)
            for k in range(4):
                step(k, k, k == 0, False)
            with pe.Fori(1, NT // 4 - 1) as i:
                k = i * 4
                for r in range(4):
                    step(k + r, r, False, False)
            for r in range(4):
                step(NT - 4 + r, r, False, r == 3)
            turn_h(NT - 1, 1)
            down(NT - 1, 1, expert(NT - 1))


def kernel(**inputs):
    import concourse.bacc as bacc
    from concourse.bass_utils import run_bass_kernel_spmd

    a = {k.replace("L0_", ""): np.asarray(v) for k, v in inputs.items()}
    tb = tables()
    wqh = a["ffn_wq"].reshape(NH, HD, C)
    wkh = np.repeat(a["ffn_wk"].reshape(NH // 2, HD, C), 2, 0)
    wvh = np.repeat(a["ffn_wv"].reshape(NH // 2, HD, C), 2, 0)

    def turned(w):
        return np.concatenate([w[:, HD // 2:], w[:, :HD // 2]], 1)

    def cols(w):
        return w.reshape(C, C).T

    arrays = {
        "x": a["x"], "adj": a["adj"], "W": a["gnn_W"], "WT": a["gnn_W"].T,
        "att_src": a["gnn_att_src"].reshape(NH, HD, 1), "att_dst": a["gnn_att_dst"].reshape(NH, HD, 1),
        "ln1": a["ffn_ln1_w"], "ln2": a["ffn_ln2_w"], "wq": cols(wqh), "wqr": cols(turned(wqh)),
        "wk": cols(wkh), "wkr": cols(turned(wkh)), "wv": cols(wvh), "wo": a["ffn_wo"].T, "router": a["ffn_router_w"].T,
        "w1": a["ffn_w1"].transpose(2, 0, 1), "w3": a["ffn_w3"].transpose(2, 0, 1), "w2": a["ffn_w2"].transpose(0, 2, 1),
        "rope_h": tb["rope"], "ident_h": tb["ident"], "causal_h": tb["causal"], "before_h": tb["before"],
        "small_h": tb["small"], "tileno_h": tb["tileno"],
    }
    arrays = {"in_" + k: np.ascontiguousarray(v) for k, v in arrays.items()}
    nc = bacc.Bacc("TRN2", target_bir_lowering=False, num_devices=1)
    args = [nc.dram_tensor(k, v.shape, mybir.dt.from_np(v.dtype), kind="ExternalInput").ap() for k, v in arrays.items()]
    out = nc.dram_tensor("out_0", (B, L, C), F32, kind="ExternalOutput").ap()
    gnn_moe_block(nc, *args, out)
    r = run_bass_kernel_spmd(nc, [arrays], core_ids=[0])
    return r.results[0]["out_0"]
```

```python
from contextlib import ExitStack

import numpy as np
import concourse.bass as bass
from concourse import mybir
from concourse.alu_op_type import AluOpType as ALU

F32 = mybir.dt.float32
BF16 = mybir.dt.bfloat16
U8 = mybir.dt.uint8
U32 = mybir.dt.uint32
I32 = mybir.dt.int32
ACT = mybir.ActivationFunctionType
AX = mybir.AxisListType

B, L, C = 128, 128, 128
NH, HD = 4, 32
NE, HID = 8, 341
GB = 4
NG = B // GB
GW, HW = HD + 2, HD + 1
SKEW = HD - 1
HC = [(0, 128), (128, 128), (256, HID - 256)]
ROW = C + 2
REGION = B + 1
NT = 2 * B + NE
TOK = B * L
BIG = float(2.0 ** 100)
RING = 8
EPS_LN, EPS_RMS, EPS_TOP = 1e-5, 1e-6, 1e-9
ROUTE = 28


ORDER = """T.yT G.xn G.h A.hN G.p1.0 T.wo A.q T.ms A.k A.kr A.v A.kk G.o1.0 T.f A.s2.0 G.p1.1 T.lg A.o2.0
G.v1.0 G.o1.1 G.p1.2 G.v1.1 A.s2.1 T.rank A.v2.0 G.o1.2 G.p1.3 A.o2.1 G.v1.2 A.s2.2 G.o1.3
A.v2.1 A.o2.2 A.s2.3 G.v1.3 N.nx A.v2.2 M.na A.o2.3 T.sc A.v2.3""".split()


def tables():
    inv = (1.0 / 10000.0 ** (np.arange(0, HD, 2, dtype=np.float32) / HD)).astype(np.float32)
    fr = np.outer(np.arange(L, dtype=np.float32), inv)
    emb = np.concatenate([fr, fr], -1)
    cos, sin = np.cos(emb).T.astype(np.float32), np.sin(emb).T.astype(np.float32)
    sin = np.concatenate([-sin[:HD // 2], sin[HD // 2:]])
    cos, sin = np.tile(cos, (NH, 1)), np.tile(sin, (NH, 1))
    scale = np.float32(1.0) / np.sqrt(np.float32(HD))
    rope = np.stack([cos * scale, sin * scale, cos, sin], 1).astype(np.float32)
    p = np.arange(128, dtype=np.float32)
    small = np.zeros((128, 3 * NE + 1 + 2 * GB), np.float32)
    small[:, 0:NE] = np.arange(NE)
    small[:, NE:2 * NE] = np.arange(NE) * REGION * L
    small[:, 2 * NE] = p
    first = np.arange(2)[:, None] * TOK + np.arange(GB)[None] * L
    small[:, 3 * NE + 1:] = p[:, None] + first.reshape(1, -1) - GB * L
    return {"rope": rope.reshape(128, 4 * L), "ident": np.eye(128, dtype=np.float32),
            "causal": np.where(np.tril(np.ones((L, L), bool)), 0.0, -BIG).astype(np.float32),
            "before": (p[:, None] < p[None]).astype(np.float32), "small": small,
            "tileno": np.arange(NT, dtype=np.float32)[None]}


def gnn_moe_block(nc, x, adj, W, WT, att_src, att_dst, ln1, ln2, wq, wqr, wk, wkr, wv, wo, router,
                  w1, w3, w2, rope_h, ident_h, causal_h, before_h, small_h, tileno_h, out):
    ctx = ExitStack()
    with ctx:
        def sb(name, shape, dt=F32):
            return ctx.enter_context(nc.sbuf_tensor(name, shape, dt))

        def sem(name):
            return ctx.enter_context(nc.semaphore(name))

        def two(name, shape, dt=F32):
            return [sb(f"{name}{i}", shape, dt) for i in range(2)]

        def dram(name, shape):
            return nc.dram_tensor(name, shape, F32, kind="Internal").ap()

        routed = dram("routed", [(NE * REGION + NE) * L, ROW])
        parts = dram("parts", [2 * TOK + 2 * NE * L, C])
        base_d = dram("base_d", [TOK, C])

        ident = sb("ident", [128, 128])
        identb = sb("identb", [128, 128], BF16)
        tmp_f = sb("tmp_f", [128, 2, 128])
        causal = sb("causal", [128, 128], BF16)
        before = sb("before", [128, 128], BF16)
        onesb = sb("onesb", [128, 128], BF16)
        rope = sb("rope", [128, 4, L])
        small = sb("small", [128, 3 * NE + 1 + 2 * GB])
        expno, region0, partno = small[:, 0:NE], small[:, NE:2 * NE], small[:, 2 * NE:2 * NE + 1]
        tileno = sb("tileno", [1, NT])
        ln1c = sb("ln1c", [C, 1])
        ln2c = sb("ln2c", [C, 1])
        half = sb("half", [128, 2, GB])
        w_oc = sb("w_oc", [C, C])
        att = sb("att", [C, 2 * NH])
        wh = sb("wh", [C, NH, HD + 1])
        wd = sb("wd", [C, NH, L])
        projw = sb("projw", [C, 4, C])
        wv_s = sb("wv_s", [C, C])
        wo_s = sb("wo_s", [C, C])
        rout = sb("rout", [C, 128])
        w1_s = sb("w1_s", [C, NE, HID])
        w3_s = sb("w3_s", [C, NE, HID])
        w2_s = sb("w2_s", [128, NE, 3, C])

        xs = two("xs", [L, GB, C])
        adj8 = two("adj8", [L, GB, L], U8)
        mask = sb("mask", [L, GB, L], BF16)
        st_g, mv_g = sb("st_g", [L, GB, 6]), sb("mv_g", [L, GB, 2])
        ve_g, rstd = sb("ve_g", [L, GB]), sb("rstd", [L, GB])
        xn, xnT = sb("xn", [L, GB, C]), sb("xnT", [C, GB, L])
        hE = sb("hE", [L, GB, NH * GW + 1])
        tb, ub = sb("tb", [L, NH, L]), two("ub", [L, NH, L])
        nm1 = sb("nm1", [L, GB, NH])
        p1, pT1 = two("p1", [L, NH, L]), two("pT1", [L, NH, L])
        ri1, og = sb("ri1", [L, GB, NH]), sb("og", [L, GB, C])
        x1 = two("x1", [L, GB, C])
        st_a, mv_a = sb("st_a", [L, GB, 6]), sb("mv_a", [L, GB, 2])
        va, rr = sb("va", [L, 2, GB]), sb("rr", [L, 2, GB])
        z, hN, hT = two("z", [L, GB, C]), sb("hN", [L, GB, C]), sb("hT", [C, GB, L])
        qa, qb, qT = sb("qa", [C, GB, L]), sb("qb", [C, GB, L]), sb("qT", [C, GB, L])
        ka, kb, kk = sb("ka", [C, GB, L]), sb("kb", [C, GB, L]), sb("kk", [C, GB, L])
        kbd = sb("kbd", [C, GB, NH, L])
        vE = sb("vE", [L, GB, NH * HW + 2])
        nm2 = sb("nm2", [L, GB, NH])
        p2, pT2 = two("p2", [L, NH, L]), two("pT2", [L, NH, L])
        ri2, y = sb("ri2", [L, GB, NH]), two("y", [L, GB, C])
        yT, x2, sq = sb("yT", [C, GB, L]), sb("x2", [L, GB, C]), sb("sq", [L, GB, C])
        ms, ve_t, r3 = sb("ms", [L, GB]), sb("ve_t", [L, GB]), sb("r3", [L, GB])
        fx = [two(f"fx{k}", [L, GB, ROW]) for k in range(2)]
        fT, bs = sb("fT", [C, GB, L]), two("bs", [L, GB, C])
        lg, mx8, ix8 = sb("lg", [L, GB, NE]), sb("mx8", [L, GB, 8]), sb("ix8", [L, GB, 8], U32)
        ixf, d8, e8 = sb("ixf", [L, 2, GB]), sb("d8", [L, GB, 8]), sb("e8", [L, GB, 8])
        se, s12, den, rden = sb("se", [L, GB]), sb("s12", [L, GB]), sb("den", [L, GB]), sb("rden", [L, GB])
        oh, ohb = sb("oh", [L, 2, GB, NE]), sb("ohb", [L, GB, NE], BF16)
        pos, mp = sb("pos", [L, GB, NE]), sb("mp", [L, 2, GB, NE])
        runc = two("runc", [128, NE])
        dcur = two("dcur", [L, 2 * GB])
        slotf = sb("slotf", [L, 2 * GB])
        slot = two("slot", [L, 2 * GB], I32)
        padx = sb("padx", [L, 2 * NE, ROW])
        cnt, cnti, nti = sb("cnt", [128, NE]), sb("cnti", [128, NE], I32), sb("nti", [128, NE], I32)
        ntf, jump, cum = sb("ntf", [128, NE]), sb("jump", [128, NE]), sb("cum", [128, NE])
        padi = sb("padi", [128, NE], I32)
        ex, tr, ty = two("ex", [1, NT]), two("tr", [1, NT]), sb("ty", [1, NT])
        exi, tri = sb("exi", [1, NT], I32), sb("tri", [1, NT], I32)
        xt = [sb(f"xt{i}", [128, ROW]) for i in range(RING)]
        ys = [sb(f"ys{i}", [128, C]) for i in range(RING)]
        xT, sg, hu, hsT = two("xT", [C, 128]), two("sg", [128, HID]), two("hu", [128, HID]), two("hsT", [128, 3, 128])
        c_in = [[x1[i], z[i], y[i]] for i in range(2)]
        c_s, c_o = [xs[0], xs[1]], [bs[0], bs[1]]

        bank = [ctx.enter_context(nc.psum_tensor(f"bank{i}", [128, 512], F32)) for i in range(8)]
        g0, g1, g2, g3, a0, a1, a3, t2 = bank
        gp = [g0, g1]
        h1_p, h3_p, x_p, hs_p, y_p = [g0, g1], [g2, g3], a0, a1, [a3, t2]

        names = """ld_c ld_w prep0 prep prep_ps half_ ready wscale xl0 xl1 al0 al1
        mask st_g mv_g ve_g rstd xn xnT_ps xnT hp_ps hE P_ps t u m1 e1 pT1_ps pT1 pv1 ri1 og x1
        st_a mv_a va norm_a z hN hT_ps hT proj qa qb qT ka kb kk kd kp vE s_ps m2 e2
        pT2_ps pT2 pv2 ri2 y yT_ps yT wo_ps x2 sq ve_t r3 fx fx1 fT_ps fT lg_ps route e8 onehot
        rank_ps base bst0 bst1 sc0 sc1 padst padsc table
        tab xtr xT h1 h3 htr sg hu hsT yp ys 
        ci0 ci1 csum cnt_ cout ost0 ost1 turn_dve turn_pool""".split()
        names += [f"{n}{r}" for n in ("xq", "zs") for r in range(RING)]
        S = {n: sem("s_" + n) for n in names}

        block = ctx.enter_context(nc.Block())

        def heads(ps, at, n):
            a = ps[:, 0:1]
            return bass.AP(a.tensor, a.offset + at, [a.ap[0], [128 + SKEW, NH], [1, n]])

        def late(v, k):
            return not isinstance(v, int) or v >= k

        def phase1(eng, steps):
            def body(g, p, on):
                shifted = {"M": steps(g + 1, 1 - p), "B": steps(g - 1, 1 - p)}
                now = steps(g, p)
                for step in ORDER:
                    stage, name, *j = step.split(".")
                    parts = shifted.get(stage, now)
                    if {"M": "G", "B": "T"}.get(stage, stage) in on and name in parts:
                        parts[name](*map(int, j))

            parts = steps(-1, 1)
            for name in ("nx",):
                if name in parts:
                    parts[name]()
            body(0, 0, "NG")
            body(1, 1, "NGA")
            body(2, 0, "NGAT")
            body(3, 1, "NGAT")
            with eng.Fori(2, NG // 2 - 1) as i:
                body(i * 2, 0, "NGAT")
                body(i * 2 + 1, 1, "NGAT")
            body(NG - 2, 0, "NGAT")
            body(NG - 1, 1, "GAT")
            body(NG, 0, "AT")
            body(NG + 1, 1, "T")

        NCONST = 17 + 2 * NH

        @block.sync
        def _(sp):
            loads = [(ident[:], ident_h), (tmp_f[:, 0, :], causal_h), (tmp_f[:, 1, :], before_h),
                     (small[:], small_h), (tileno[:], tileno_h), (rope[:].rearrange("p a b -> p (a b)"), rope_h),
                     (ln1c[:], ln1.rearrange("(c a) -> c a", a=1)), (ln2c[:], ln2.rearrange("(c a) -> c a", a=1)),
                     (w_oc[:], W), (wv_s[:], wv), (wo_s[:], wo), (wh[:, :, 0:HD], WT.rearrange("c (h d) -> c h d", h=NH))]
            loads += [(projw[:, i, :], s) for i, s in enumerate((wq, wqr, wk, wkr))]
            for d, s in loads:
                sp.dma_start(d, s).then_inc(S["ld_c"], 16)
            sp.wait_ge(S["prep0"], 2)
            sp.dma_start(rout[:, 0:NE], router).then_inc(S["ld_c"], 16)
            for h in range(NH):
                sp.dma_start(att[h * HD:(h + 1) * HD, h:h + 1], att_src[h]).then_inc(S["ld_c"], 16)
                sp.dma_start(att[h * HD:(h + 1) * HD, NH + h:NH + h + 1], att_dst[h]).then_inc(S["ld_c"], 16)
            assert len(loads) + 1 + 2 * NH == NCONST

            def steps(g, p):
                def nx():
                    n, q = g + 1, 1 - p
                    if late(n, 2):
                        sp.wait_ge(S["x1"], 4 * (n - 1))
                        sp.wait_ge(S["mask"], n - 1)
                    sp.dma_start(xs[q][:], x[bass.ds(n * GB, GB)].rearrange("b l c -> l b c")).then_inc(S[f"xl{q}"], 16)
                    sp.dma_start(adj8[q][:], adj[bass.ds(n * GB, GB)].rearrange("b l c -> l b c")).then_inc(S[f"al{q}"], 16)
                    if isinstance(n, int) and n == 1:
                        sp.dma_start(w1_s[:], w1).then_inc(S["ld_w"], 16)
                        sp.dma_start(w3_s[:], w3).then_inc(S["ld_w"], 16)
                        for c, (o, m) in enumerate(HC):
                            sp.dma_start(w2_s[0:m, :, c, :], w2[:, o:o + m, :].rearrange("e p c -> p e c")).then_inc(S["ld_w"], 16)
                        sp.wait_ge(S["ready"], 2)
                        sp.dma_start(routed[NE * REGION * L:, :].rearrange("(i p) c -> p i c", p=L),
                                     padx[:, NE:2 * NE, :]).then_inc(S["padst"], 16)

                def f():
                    t = g - 2
                    sp.wait_ge(S["base"], t + 1)
                    sp.dma_start(base_d[bass.ds(t * GB * L, GB * L), :].rearrange("(b l) c -> l b c", l=L),
                                 bs[p][:]).then_inc(S[f"bst{p}"], 16)

                return {"nx": nx, "f": f}

            phase1(sp, steps)

            sp.wait_ge(S["table"], 1)
            sp.wait_ge(S["padst"], 16)
            sp.wait_ge(S["sc0"], 8 * 16 * NG // 2)
            sp.wait_ge(S["sc1"], 8 * 16 * NG // 2)
            sp.wait_ge(S["padsc"], 16 * NE)
            by_tile = routed.rearrange("(n p) c -> n p c", p=L)

            def load_tile(k, r):
                tile = sp.value_load(tri[0:1, bass.ds(k + r, 1)], min_val=0, max_val=NE * REGION + NE - 1)
                if late(k, RING):
                    sp.wait_ge(S[f"zs{r}"], 16 // RING * k)
                sp.dma_start(xt[r][:], by_tile[bass.ds(tile, 1)].rearrange("a p c -> p (a c)")).then_inc(S[f"xq{r}"], 16)

            for r in range(RING):
                load_tile(0, r)
            with sp.Fori(1, NT // RING) as i:
                for r in range(RING):
                    load_tile(i * RING, r)

            sp.wait_ge(S["bst0"], 16 * (NG // 2))
            sp.wait_ge(S["bst1"], 16 * (NG // 2))
            for r in range(RING):
                sp.wait_ge(S[f"zs{r}"], 16 * NT // RING)
            srcs = [base_d.rearrange("(b l) c -> l b c", l=L)] + [
                parts[i * TOK:(i + 1) * TOK, :].rearrange("(b l) c -> l b c", l=L) for i in range(2)]

            def load_parts(g, p):
                if late(g, 2):
                    sp.wait_ge(S["cout"], g - 1)
                for d, s in zip(c_in[p], srcs):
                    sp.dma_start(d[:], s[:, bass.ds(g * GB, GB), :]).then_inc(S[f"ci{p}"], 16)

            load_parts(0, 0)
            load_parts(1, 1)
            with sp.Fori(1, NG // 2) as i:
                for p in range(2):
                    load_parts(i * 2 + p, p)

        @block.gpsimd
        def _(pool):
            pool.memset(att[:], 0.0).then_inc(S["prep0"], 1)
            pool.memset(rout[:], 0.0).then_inc(S["prep0"], 1)
            pool.memset(half[:], -0.5).then_inc(S["half_"], 1)
            pool.memset(hE[:], 1.0).then_inc(S["ready"], 0 + 1)
            pool.memset(padx[:], 0.0).then_inc(S["prep0"], 1)
            pool.wait_ge(S["prep0"], 3)
            pool.iota(padx[:, :, C].bitcast(I32), pattern=[[L, 2 * NE]], base=2 * TOK,
                      channel_multiplier=1).then_inc(S["ready"], 1)
            pool.memset(vE[:], 1.0).then_inc(S["ready"], 1)
            pool.memset(kbd[:], 0.0).then_inc(S["ready"], 1)
            pool.wait_ge(S["half_"], 1)
            pool.wait_ge(S["ready"], 4)

            def steps(g, p):
                a, t = g - 1, g - 2

                def nx():
                    n, q = g + 1, 1 - p
                    pool.wait_ge(S[f"al{q}"], (n - q) * 8 + 16)
                    if late(n, 1):
                        pool.wait_ge(S["P_ps"], 4 * n)
                    pool.sem_inc(S["turn_pool"], 1)
                    pool.tensor_scalar(mask[:], adj8[q][:], BIG, -BIG, ALU.mult, ALU.add).then_inc(S["mask"], 1)
                    if late(n, 1):
                        pool.wait_ge(S["xn"], 4 * n)
                    pool.wait_ge(S["ve_g"], n + 1)
                    pool.tensor_tensor(rstd[:], ve_g[:], half[:, 0, :], ALU.pow).then_inc(S["rstd"], 1)

                def na():
                    pool.wait_ge(S["va"], a + 1)
                    if late(a, 1):
                        pool.wait_ge(S["hN"], 4 * a)
                    pool.tensor_tensor(rr[:], va[:], half[:], ALU.pow).then_inc(S["norm_a"], 1)

                def ms_():
                    if late(t, 1):
                        pool.wait_ge(S["fx"], 4 * t)
                        pool.wait_ge(S["fx1"], t)
                    pool.wait_ge(S["ve_t"], t + 1)
                    pool.tensor_tensor(r3[:], ve_t[:], half[:, 0, :], ALU.pow).then_inc(S["r3"], 1)
                    if late(t, 2):
                        pool.wait_ge(S[f"bst{p}"], 8 * (t - p))
                    pool.wait_ge(S["x2"], t + 1)
                    pool.tensor_tensor(bs[p][:], x1[p][:], x2[:], ALU.add).then_inc(S["base"], 1)

                def v1(j):
                    pool.wait_ge(S["og"], 4 * g + j + 1)
                    if j == 0 and late(g, 2):
                        pool.wait_ge(S["hN"], 4 * (g - 1))
                        pool.wait_ge(S["base"], g - 1)
                    pool.tensor_tensor(x1[p][:, j, :], xs[p][:, j, :], og[:, j, :], ALU.add).then_inc(S["x1"], 1)

                def sc():
                    pool.wait_ge(S["route"], ROUTE * t + ROUTE)
                    pool.wait_ge(S["fx1"], t + 1)
                    pool.sem_inc(S["turn_pool"], 1)
                    for k in range(2):
                        for j in range(GB):
                            i = k * GB + j
                            pool.indirect_dma_start(routed, bass.IndirectOffsetOnAxis(slot[p][:, i:i + 1], 0),
                                                    fx[k][p][:, j, :], None).then_inc(S[f"sc{p}"], 16)

                return {"nx": nx, "na": na, "ms": ms_, "v1": v1, "sc": sc}

            phase1(pool, steps)
            pool.wait_ge(S["tab"], 1)
            for e in range(NE):
                pool.indirect_dma_start(routed, bass.IndirectOffsetOnAxis(padi[:, e:e + 1], 0),
                                        padx[:, e, :], None).then_inc(S["padsc"], 16)
            with pool.Fori(0, NT // RING) as i:
                k = i * RING
                for r in range(RING):
                    pool.wait_ge(S["ys"], k + r + 1)
                    pool.sem_inc(S["turn_pool"], 1)
                    pool.indirect_dma_start(parts, bass.IndirectOffsetOnAxis(xt[r][:, C:C + 1].bitcast(I32), 0),
                                            ys[r][:], None).then_inc(S[f"zs{r}"], 16)

        @block.scalar
        def _(act):
            def steps(g, p):
                a, t = g - 1, g - 2

                def yT_():
                    act.wait_ge(S["yT_ps"], t + 1)
                    if late(t, 1):
                        act.wait_ge(S["wo_ps"], t)
                    act.activation(yT[:].rearrange("c b l -> c (b l)"), t2[:], ACT.Copy).then_inc(S["yT"], 1)

                def xn_():
                    act.wait_ge(S["xnT_ps"], g + 1)
                    if late(g, 1):
                        act.wait_ge(S["P_ps"], 4 * g)
                    act.activation(xnT[:].rearrange("c b l -> c (b l)"), g3[:], ACT.Copy).then_inc(S["xnT"], 1)

                def hN_():
                    act.wait_ge(S["hT_ps"], a + 1)
                    if late(a, 1):
                        act.wait_ge(S["proj"], 5 * a)
                    act.activation(hT[:].rearrange("c b l -> c (b l)"), a3[:], ACT.Copy).then_inc(S["hT"], 1)

                def h():
                    act.wait_ge(S["hp_ps"], g + 1)
                    if late(g, 1):
                        act.wait_ge(S["pv1"], 4 * g)
                        act.wait_ge(S["t"], 4 * g)
                    for i in range(2):
                        act.activation(hE[:, 2 * i:2 * i + 2, 0:NH * GW].rearrange("p b (h w) -> p b h w", w=GW)[:, :, :, 0:HD + 1],
                                       gp[i][:, 0:2 * NH * (HD + 1)].rearrange("p (b h w) -> p b h w", b=2, h=NH),
                                       ACT.Copy).then_inc(S["hE"], 1)

                def v():
                    act.wait_ge(S["proj"], 5 * a + 5)
                    if late(a, 1):
                        act.wait_ge(S["pv2"], 4 * a)
                    act.activation(vE[:, :, 0:NH * HW].rearrange("p b (h w) -> p b h w", w=HW)[:, :, :, 0:HD],
                                   a1[:].rearrange("p (b h w) -> p b h w", b=GB, h=NH), ACT.Copy).then_inc(S["vE"], 1)

                def kk_():
                    act.wait_ge(S["kk"], a + 1)
                    if late(a, 1):
                        act.wait_ge(S["s_ps"], 4 * a)
                    for h in (2, 3):
                        o = slice(h * HD, (h + 1) * HD)
                        act.activation(kbd[o, :, h, :], kk[o, :, :], ACT.Copy).then_inc(S["kp"], 1)

                def wo_():
                    act.wait_ge(S["x2"], t + 1)
                    if late(t, 1):
                        act.wait_ge(S["ve_t"], t)
                        act.wait_ge(S["sq"], t)
                    for j in range(GB):
                        last = act.activation(sq[:, j, :], x2[:, j, :], ACT.Square, accum_out=ms[:, j:j + 1])
                    last.then_inc(S["sq"], 1)

                def f_():
                    act.wait_ge(S["fT_ps"], t + 1)
                    if late(t, 1):
                        act.wait_ge(S["lg_ps"], t)
                    act.activation(fT[:].rearrange("c b l -> c (b l)"), t2[:], ACT.Copy).then_inc(S["fT"], 1)
                    if late(t, 2):
                        act.wait_ge(S[f"sc{p}"], 64 * (t - p))
                    for j in range(GB):
                        last = act.activation(fx[1][p][:, j, 0:C], x2[:, j, :], ACT.Copy, scale=r3[:, j:j + 1])
                    last.then_inc(S["fx1"], 1)

                def lg_():
                    act.wait_ge(S["route"], ROUTE * t + 10)
                    act.activation(e8[:], d8[:], ACT.Exp).then_inc(S["e8"], 1)

                def exp1(j):
                    act.wait_ge(S["m1"], 4 * g + j + 1)
                    if late(g, 1) or j >= 2:
                        act.wait_ge(S["pT1_ps"], 4 * g + j - 1)
                    for h in range(NH):
                        last = act.activation(p1[j % 2][:, h, :], ub[j % 2][:, h, :], ACT.Exp, bias=nm1[:, j, h:h + 1])
                    last.then_inc(S["e1"], 1)

                def exp2(j):
                    act.wait_ge(S["m2"], 4 * a + j + 1)
                    if late(a, 1) or j >= 2:
                        act.wait_ge(S["pT2_ps"], 4 * a + j - 1)
                    for h in range(NH):
                        last = act.activation(p2[j % 2][:, h, :], a0[:, h * L:(h + 1) * L], ACT.Exp, bias=nm2[:, j, h:h + 1])
                    last.then_inc(S["e2"], 1)

                def out1(j):
                    act.wait_ge(S["pT1_ps"], 4 * g + j + 1)
                    if late(g, 1) or j >= 2:
                        act.wait_ge(S["pv1"], 4 * g + j - 1)
                    act.activation(pT1[j % 2][:].rearrange("c b l -> c (b l)"), g2[:], ACT.Copy).then_inc(S["pT1"], 1)

                def out2(j):
                    act.wait_ge(S["pT2_ps"], 4 * a + j + 1)
                    if late(a, 1) or j >= 2:
                        act.wait_ge(S["pv2"], 4 * a + j - 1)
                    act.activation(pT2[j % 2][:].rearrange("c b l -> c (b l)"), a1[:], ACT.Copy).then_inc(S["pT2"], 1)

                def rank():
                    if isinstance(g, int) and g == 2:
                        act.wait_ge(S["ld_w"], 16 * 5)
                        act.activation(w1_s[:], w1_s[:], ACT.Copy, scale=ln2c[:]).then_inc(S["wscale"], 1)
                        act.activation(w3_s[:], w3_s[:], ACT.Copy, scale=ln2c[:]).then_inc(S["wscale"], 1)

                return {"yT": yT_, "xn": xn_, "hN": hN_, "h": h, "v": v, "kk": kk_, "wo": wo_, "f": f_, "lg": lg_, "rank": rank,
                        "p1": exp1, "s2": exp2, "o1": out1, "o2": out2}

            act.wait_ge(S["ready"], 4)
            act.wait_ge(S["prep"], 1)
            phase1(act, steps)

            def gate(k, q):
                act.wait_ge(S["h1"], k + 1)
                if late(k, 2):
                    act.wait_ge(S["hu"], k - 1)
                act.activation(sg[q][:], h1_p[q][:, 0:HID], ACT.Silu).then_inc(S["sg"], 1)

            def out_h(k, q):
                act.wait_ge(S["htr"], k + 1)
                if late(k, 2):
                    act.wait_ge(S["yp"], k - 1)
                act.activation(hsT[q][:, 0:2, :].rearrange("p a b -> p (a b)"), hs_p[:, 0:256], ACT.Copy)
                act.activation(hsT[q][0:HC[2][1], 2, :], hs_p[0:HC[2][1], 256:384], ACT.Copy).then_inc(S["hsT"], 1)

            gate(0, 0)
            gate(1, 1)
            out_h(0, 0)
            with act.Fori(1, NT // 2) as i:
                k = i * 2
                for q in range(2):
                    gate(k + q, q)
                    out_h(k + q - 1, 1 - q)
            out_h(NT - 1, 1)

            with act.Fori(0, NG // 2) as i:
                g = i * 2
                for p in range(2):
                    act.wait_ge(S["cout"], g + p + 1)
                    act.dma_start(out[bass.ds((g + p) * GB, GB)].rearrange("b l c -> l b c"), c_o[p][:]).then_inc(S[f"ost{p}"], 16)
            act.wait_ge(S["ost0"], 16 * (NG // 2))
            act.wait_ge(S["ost1"], 16 * (NG // 2))

        @block.vector
        def _(dve):
            dve.wait_ge(S["ld_c"], 16 * NCONST)
            dve.wait_ge(S["prep0"], 2)
            dve.memset(onesb[:], 1.0)
            dve.tensor_copy(identb[:], ident[:])
            dve.tensor_copy(causal[:], tmp_f[:, 0, :])
            dve.tensor_copy(before[:], tmp_f[:, 1, :])
            dve.tensor_copy(runc[1][:], region0)
            dve.tensor_copy(dcur[1][:], small[:, 3 * NE + 1:])
            dve.tensor_scalar(projw[:], projw[:], ln1c[:], None, ALU.mult)
            dve.tensor_scalar(wv_s[:], wv_s[:], ln1c[:], None, ALU.mult)
            dve.tensor_scalar(rout[:], rout[:], ln2c[:], None, ALU.mult)
            dve.wait_ge(S["prep_ps"], 1)
            dve.tensor_copy(wh[:, :, HD], a0[:, 0:NH])
            dve.tensor_copy(wd[:], a0[:, NH:2 * NH].unsqueeze(2).broadcast_to([C, NH, L])).then_inc(S["prep"], 1)
            dve.wait_ge(S["prep"], 1)
            dve.wait_ge(S["ready"], 4)

            def steps(g, p):
                a, t, pa = g - 1, g - 2, 1 - p
                n_route = [0]

                def link(ins, last=True):
                    n_route[0] += 1
                    ins.then_inc(S["route"], 1)
                    if last:
                        dve.wait_ge(S["route"], ROUTE * t + n_route[0])

                def nx():
                    n, q = g + 1, 1 - p
                    dve.wait_ge(S[f"xl{q}"], (n - q) * 8 + 16)
                    if late(n, 1):
                        dve.wait_ge(S["rstd"], n)
                        dve.wait_ge(S["xn"], 4 * n)
                    for j in range(GB):
                        dve.bn_stats(st_g[:, j, :], xs[q][:, j, :]).then_inc(S["st_g"], 1)
                    for j in range(GB):
                        dve.wait_ge(S["st_g"], 4 * n + j + 1)
                        dve.sem_inc(S["turn_dve"], 1)
                        dve.bn_aggr(mv_g[:, j, :], st_g[:, j, :]).then_inc(S["mv_g"], 1)
                    dve.wait_ge(S["mv_g"], 4 * n + 4)
                    dve.tensor_scalar(ve_g[:], mv_g[:, :, 1], EPS_LN, None, ALU.add).then_inc(S["ve_g"], 1)

                def na():
                    dve.wait_ge(S["x1"], 4 * a + 4)
                    if late(a, 1):
                        dve.wait_ge(S["norm_a"], a)
                        dve.wait_ge(S["hN"], 4 * a)
                    for j in range(GB):
                        dve.bn_stats(st_a[:, j, :], x1[pa][:, j, :]).then_inc(S["st_a"], 1)
                    for j in range(GB):
                        dve.wait_ge(S["st_a"], 4 * a + j + 1)
                        dve.sem_inc(S["turn_dve"], 1)
                        dve.bn_aggr(mv_a[:, j, :], st_a[:, j, :]).then_inc(S["mv_a"], 1)
                    dve.wait_ge(S["mv_a"], 4 * a + 4)
                    v = mv_a[:, :, 1]
                    dve.tensor_scalar(va[:, 0, :], v, EPS_LN, None, ALU.add)
                    dve.tensor_scalar(va[:, 1, :], v, 1.0 + EPS_RMS, EPS_RMS * EPS_LN, ALU.mult, ALU.add).then_inc(S["va"], 1)

                def xn_():
                    dve.wait_ge(S["rstd"], g + 1)
                    if late(g, 1):
                        dve.wait_ge(S["xnT_ps"], g)
                    for j in range(GB):
                        dve.tensor_scalar(xn[:, j, :], xs[p][:, j, :], mv_g[:, j, 0:1], rstd[:, j:j + 1],
                                          ALU.subtract, ALU.mult).then_inc(S["xn"], 1)

                def hN_():
                    dve.wait_ge(S["norm_a"], a + 1)
                    if late(a, 1):
                        dve.wait_ge(S["hT_ps"], a)
                    if late(a, 2):
                        dve.wait_ge(S["x2"], a - 1)
                    for j in range(GB):
                        dve.tensor_scalar(hN[:, j, :], x1[pa][:, j, :], mv_a[:, j, 0:1], rr[:, 1, j:j + 1],
                                          ALU.subtract, ALU.mult)
                        dve.tensor_scalar(z[pa][:, j, :], x1[pa][:, j, :], mv_a[:, j, 0:1], rr[:, 0, j:j + 1],
                                          ALU.subtract, ALU.mult).then_inc(S["hN"], 1)

                def wo_():
                    dve.wait_ge(S["wo_ps"], t + 1)
                    if late(t, 1):
                        dve.wait_ge(S["base"], t)
                        dve.wait_ge(S["fx1"], t)
                    dve.tensor_tensor(x2[:].rearrange("p b c -> p (b c)"), t2[:],
                                      z[p][:].rearrange("p b c -> p (b c)"), ALU.add).then_inc(S["x2"], 1)

                def ms_():
                    dve.wait_ge(S["sq"], t + 1)
                    if late(t, 1):
                        dve.wait_ge(S["r3"], t)
                    dve.tensor_scalar(ve_t[:], ms[:], 1.0 / C, EPS_RMS, ALU.mult, ALU.add).then_inc(S["ve_t"], 1)

                def f_():
                    dve.wait_ge(S["r3"], t + 1)
                    if late(t, 2):
                        dve.wait_ge(S[f"sc{p}"], 64 * (t - p))
                    for j in range(GB):
                        dve.tensor_scalar(fx[0][p][:, j, 0:C], x2[:, j, :], r3[:, j:j + 1], None,
                                          ALU.mult).then_inc(S["fx"], 1)

                def turn(dst, src, i, n):
                    dve.wait_ge(S["proj"], 5 * a + n)
                    return dve.tensor_tensor(dst[:], src[:].rearrange("c (b l) -> c b l", b=GB),
                                             rope[:, i, :].unsqueeze(1).broadcast_to([C, GB, L]), ALU.mult)

                def q_():
                    if late(a, 1):
                        dve.wait_ge(S["s_ps"], 4 * a)
                        dve.wait_ge(S["kp"], 2 * a)
                        dve.wait_ge(S["kd"], 2 * a)
                    turn(qa, a0, 0, 1).then_inc(S["qa"], 1)
                    turn(qb, a1, 1, 2).then_inc(S["qb"], 1)
                    dve.wait_ge(S["qa"], a + 1)
                    dve.wait_ge(S["qb"], a + 1)
                    dve.tensor_tensor(qT[:], qa[:], qb[:], ALU.add).then_inc(S["qT"], 1)

                def k_():
                    turn(ka, a3, 2, 3).then_inc(S["ka"], 1)

                def kr_():
                    turn(kb, a0, 3, 4).then_inc(S["kb"], 1)

                def kk_():
                    dve.wait_ge(S["ka"], a + 1)
                    dve.wait_ge(S["kb"], a + 1)
                    dve.tensor_tensor(kk[:], ka[:], kb[:], ALU.add).then_inc(S["kk"], 1)
                    dve.wait_ge(S["kk"], a + 1)
                    for h in (0, 1):
                        o = slice(h * HD, (h + 1) * HD)
                        dve.tensor_copy(kbd[o, :, h, :], kk[o, :, :]).then_inc(S["kd"], 1)

                def scores1(j):
                    dve.wait_ge(S["P_ps"], 4 * g + j + 1)
                    dve.wait_ge(S["hE"], 2 * g + 2)
                    if late(g, 1) or j:
                        dve.wait_ge(S["u"], 4 * g + j)
                    dve.tensor_tensor(tb[:], gp[j % 2][:].rearrange("p (h l) -> p h l", h=NH),
                                      hE[:, j, 0:NH * GW].rearrange("p (h w) -> p h w", w=GW)[:, :, HD:HD + 1].broadcast_to([L, NH, L]),
                                      ALU.add).then_inc(S["t"], 1)
                    dve.wait_ge(S["t"], 4 * g + j + 1)
                    if late(g, 1) or j >= 2:
                        dve.wait_ge(S["e1"], 4 * g + j - 1)
                    u = ub[j % 2]
                    dve.scalar_tensor_tensor(out=u[:].rearrange("p h l -> p (h l)"), in0=tb[:].rearrange("p h l -> p (h l)"), scalar=0.2,
                                             in1=tb[:].rearrange("p h l -> p (h l)"), op0=ALU.mult, op1=ALU.max).then_inc(S["u"], 1)
                    dve.wait_ge(S["u"], 4 * g + j + 1)
                    if late(g, 1) and j == 0:
                        dve.wait_ge(S["e1"], 4 * g)
                    dve.tensor_reduce(nm1[:, j, :], u[:], AX.X, ALU.max, negate=True).then_inc(S["m1"], 1)

                def max2(j):
                    dve.wait_ge(S["s_ps"], 4 * a + j + 1)
                    if late(a, 1) and j == 0:
                        dve.wait_ge(S["e2"], 4 * a)
                    dve.tensor_reduce(nm2[:, j, :], a0[:].rearrange("p (h l) -> p h l", h=NH), AX.X, ALU.max,
                                      negate=True).then_inc(S["m2"], 1)

                def mix(j, ps, pv, ri, s_ri, dst, s_dst, one, n):
                    dve.wait_ge(S[pv], 4 * n + j + 1)
                    dve.reciprocal(ri[:, j, :], heads(ps, one, 1).rearrange("p h a -> p (h a)")).then_inc(S[s_ri], 1)
                    dve.wait_ge(S[s_ri], 4 * n + j + 1)
                    dve.tensor_tensor(dst[:, j, :].rearrange("p (h d) -> p h d", h=NH), heads(ps, 0, HD),
                                      ri[:, j, :].unsqueeze(2).broadcast_to([L, NH, HD]), ALU.mult).then_inc(S[s_dst], 1)

                def mix1(j):
                    if late(g, 1) and j == 0:
                        dve.wait_ge(S["x1"], 4 * g)
                    mix(j, g3, "pv1", ri1, "ri1", og, "og", GW - 1, g)

                def mix2(j):
                    if late(a, 2) and j == 0:
                        dve.wait_ge(S["yT_ps"], a - 1)
                    mix(j, a3, "pv2", ri2, "ri2", y[pa], "y", HD, a)

                def route1():
                    dve.wait_ge(S["lg_ps"], t + 1)
                    link(dve.tensor_copy(lg[:], t2[:].rearrange("p (b n) -> p b n", b=GB)[:, :, 0:NE]))
                    dve.sem_inc(S["turn_dve"], 1)
                    for j in range(GB):
                        link(dve.max(mx8[:, j, :], lg[:, j, :]), j == GB - 1)
                    dve.sem_inc(S["turn_dve"], 1)
                    for j in range(GB):
                        link(dve.max_index(ix8[:, j, :], mx8[:, j, :], lg[:, j, :]), j == GB - 1)
                    if late(t, 1):
                        dve.wait_ge(S["e8"], t)
                    link(dve.tensor_tensor(d8[:], mx8[:], mx8[:, :, 0:1].broadcast_to([L, GB, 8]), ALU.subtract), False)
                    link(dve.tensor_copy(ixf[:].rearrange("p k b -> p b k"), ix8[:, :, 0:2]))
                    n8 = 2 * GB
                    link(dve.tensor_tensor(oh[:].rearrange("p k b e -> p (k b) e"), expno.unsqueeze(1).broadcast_to([L, n8, NE]),
                                           ixf[:].rearrange("p k b -> p (k b)").unsqueeze(2).broadcast_to([L, n8, NE]), ALU.is_equal))
                    if late(t, 1):
                        dve.wait_ge(S["rank_ps"], t)
                    link(dve.tensor_tensor(ohb[:], oh[:, 0], oh[:, 1], ALU.add), False)
                    dve.wait_ge(S["e8"], t + 1)
                    link(dve.tensor_reduce(se[:], e8[:], AX.X, ALU.add), False)
                    link(dve.tensor_tensor(s12[:], e8[:, :, 0], e8[:, :, 1], ALU.add))
                    link(dve.scalar_tensor_tensor(out=den[:], in0=se[:], scalar=EPS_TOP, in1=s12[:], op0=ALU.mult, op1=ALU.add))
                    link(dve.reciprocal(rden[:], den[:]))
                    for k in range(2):
                        link(dve.tensor_tensor(fx[k][p][:, :, C + 1], e8[:, :, k], rden[:], ALU.mult), k == 1)
                    link(dve.tensor_scalar(dcur[p][:], dcur[1 - p][:], float(GB * L), None, ALU.add))
                    for k in range(2):
                        link(dve.tensor_copy(fx[k][p][:, :, C].bitcast(I32), dcur[p][:, k * GB:(k + 1) * GB]), k == 1)

                def route2():
                    dve.wait_ge(S["rank_ps"], t + 1)
                    link(dve.tensor_tensor(pos[:], t2[:, 0:GB * NE].rearrange("p (b e) -> p b e", e=NE),
                                           runc[1 - p][:].unsqueeze(1).broadcast_to([L, GB, NE]), ALU.add), False)
                    link(dve.tensor_tensor(runc[p][:], t2[:, GB * NE:(GB + 1) * NE], runc[1 - p][:], ALU.add))
                    for k in range(2):
                        link(dve.tensor_tensor(mp[:, k], oh[:, k], pos[:], ALU.mult), k == 1)
                    link(dve.tensor_reduce(slotf[:], mp[:].rearrange("p k b e -> p (k b) e"), AX.X, ALU.add))
                    link(dve.tensor_copy(slot[p][:], slotf[:]))

                return {"nx": nx, "na": na, "xn": xn_, "hN": hN_, "wo": wo_, "ms": ms_, "f": f_, "q": q_, "k": k_, "kr": kr_, "kk": kk_, "lg": route1,
                        "rank": route2, "p1": scores1, "s2": max2, "v1": mix1, "v2": mix2}

            phase1(dve, steps)

            steps = [0]

            def link(ins):
                steps[0] += 1
                ins.then_inc(S["csum"], 1)
                dve.wait_ge(S["csum"], steps[0])

            end = runc[(NG - 1) % 2]
            link(dve.tensor_scalar(padi[:], end[:], partno, None, ALU.add))
            dve.nop().then_inc(S["tab"], 1)
            link(dve.tensor_tensor(cnt[:], end[:], region0, ALU.subtract))
            link(dve.tensor_scalar(cnti[:], cnt[:], float(L - 1), None, ALU.add))
            link(dve.tensor_scalar(nti[:], cnti[:], 7, None, ALU.arith_shift_right))
            link(dve.tensor_copy(ntf[:], nti[:]))
            link(dve.tensor_scalar(jump[:], ntf[:], -1.0, float(REGION), ALU.mult, ALU.add))
            link(dve.tensor_copy(cum[:, 0:1], ntf[:, 0:1]))
            for e in range(1, NE):
                link(dve.tensor_tensor(cum[:, e:e + 1], cum[:, e - 1:e], ntf[:, e:e + 1], ALU.add))
            link(dve.memset(ex[0][:], 0.0))
            link(dve.tensor_copy(tr[0][:], tileno[:]))
            for e in range(NE):
                i, o = e % 2, 1 - e % 2
                link(dve.scalar_tensor_tensor(out=ex[o][:], in0=tileno[:], scalar=cum[0:1, e:e + 1], in1=ex[i][:],
                                              op0=ALU.is_ge, op1=ALU.add))
                link(dve.tensor_scalar(ty[:], tileno[:], cum[0:1, e:e + 1], jump[0:1, e:e + 1], ALU.is_ge, ALU.mult))
                link(dve.tensor_tensor(tr[o][:], tr[i][:], ty[:], ALU.add))
            link(dve.tensor_scalar(exi[:], ex[0][:], float(NE - 1), None, ALU.min))
            link(dve.tensor_copy(tri[:], tr[0][:]))
            dve.nop().then_inc(S["table"], 1)

            def out_x(k, q):
                dve.wait_ge(S["xtr"], k + 1)
                if late(k, 2):
                    dve.wait_ge(S["h3"], k - 1)
                dve.tensor_copy(xT[q][:], x_p[:, 0:128]).then_inc(S["xT"], 1)

            def gated(k, q):
                dve.wait_ge(S["h3"], k + 1)
                dve.wait_ge(S["sg"], k + 1)
                if late(k, 2):
                    dve.wait_ge(S["htr"], k - 1)
                dve.tensor_tensor(hu[q][:], h3_p[q][:, 0:HID], sg[q][:], ALU.mult).then_inc(S["hu"], 1)

            def weigh(k, r):
                dve.wait_ge(S["yp"], k + 1)
                if late(k, RING):
                    dve.wait_ge(S[f"zs{r}"], 16 // RING * (k - r))
                dve.tensor_scalar(ys[r][:], y_p[r % 2][:, 0:C], xt[r][:, C + 1:C + 2], None, ALU.mult).then_inc(S["ys"], 1)

            def step(k, r, late2=True, last=False):
                if not last:
                    out_x(k + 1, (r + 1) % 2)
                gated(k, r % 2)
                if late2:
                    weigh(k - 2, (r - 2) % RING)

            out_x(0, 0)
            for k in range(2 * RING):
                step(k, k % RING, late2=k >= 2)
            with dve.Fori(2, NT // RING - 1) as i:
                for r in range(RING):
                    step(i * RING + r, r)
            for r in range(RING):
                step(NT - RING + r, r, last=r == RING - 1)
            for k in (NT - 2, NT - 1):
                weigh(k, k % RING)

            def total(g, p):
                dve.wait_ge(S[f"ci{p}"], 24 * (g - p) + 48)
                b_, y0, y1 = c_in[p]
                if late(g, 2):
                    dve.wait_ge(S[f"ost{p}"], 8 * (g - p))
                dve.tensor_tensor(c_s[p][:], y0[:], y1[:], ALU.add).then_inc(S["cnt_"], 1)
                dve.wait_ge(S["cnt_"], g + 1)
                dve.tensor_tensor(c_o[p][:], c_s[p][:], b_[:], ALU.add).then_inc(S["cout"], 1)

            total(0, 0)
            total(1, 1)
            with dve.Fori(1, NG // 2) as i:
                for p in range(2):
                    total(i * 2 + p, p)

        @block.tensor
        def _(pe):
            pe.wait_ge(S["ld_c"], 16 * NCONST)
            pe.matmul(a0[:, 0:2 * NH], w_oc[:], att[:], start=True, stop=True).then_inc(S["prep_ps"], 1)
            pe.wait_ge(S["prep"], 1)
            pe.wait_ge(S["ready"], 4)

            def flip(ps, src, n=GB):
                for j in range(n):
                    last = pe.transpose(ps[:, j * 128:(j + 1) * 128], src[:, j, 0:128], ident[:])
                return last

            def steps(g, p):
                a, t, pa = g - 1, g - 2, 1 - p

                def yT_():
                    pe.wait_ge(S["y"], 4 * t + 4)
                    if late(t, 1):
                        pe.wait_ge(S["route"], ROUTE * t)
                    flip(t2, y[p]).then_inc(S["yT_ps"], 1)

                def xn_():
                    pe.wait_ge(S["xn"], 4 * g + 4)
                    if late(g, 1):
                        pe.wait_ge(S["og"], 4 * g)
                    flip(g3, xn).then_inc(S["xnT_ps"], 1)

                def hN_():
                    pe.wait_ge(S["hN"], 4 * a + 4)
                    if late(a, 1):
                        pe.wait_ge(S["y"], 4 * a)
                    flip(a3, hN).then_inc(S["hT_ps"], 1)

                def wo_():
                    pe.wait_ge(S["yT"], t + 1)
                    for j in range(GB):
                        last = pe.matmul(t2[:, j * C:(j + 1) * C], yT[:, j, :], wo_s[:], start=True, stop=True)
                    last.then_inc(S["wo_ps"], 1)

                def h_():
                    pe.wait_ge(S["xnT"], g + 1)
                    if late(g, 1):
                        pe.wait_ge(S["t"], 4 * g)
                    w = NH * (HD + 1)
                    for j in range(GB):
                        last = pe.matmul(gp[j // 2][:, (j % 2) * w:(j % 2 + 1) * w], xnT[:, j, :],
                                         wh[:].rearrange("c h w -> c (h w)"), start=True, stop=True)
                    last.then_inc(S["hp_ps"], 1)

                hTf = hT[:].rearrange("c b l -> c (b l)")

                def q_():
                    pe.wait_ge(S["hT"], a + 1)
                    if late(a, 1):
                        pe.wait_ge(S["e2"], 4 * a)
                        pe.wait_ge(S["pT2"], 4 * a)
                    pe.matmul(a0[:], projw[:, 0, :], hTf, start=True, stop=True).then_inc(S["proj"], 1)
                    pe.matmul(a1[:], projw[:, 1, :], hTf, start=True, stop=True).then_inc(S["proj"], 1)

                def k_():
                    pe.matmul(a3[:], projw[:, 2, :], hTf, start=True, stop=True).then_inc(S["proj"], 1)

                def kr_():
                    pe.wait_ge(S["qa"], a + 1)
                    pe.matmul(a0[:], projw[:, 3, :], hTf, start=True, stop=True).then_inc(S["proj"], 1)

                def v_():
                    pe.wait_ge(S["qb"], a + 1)
                    for j in range(GB):
                        last = pe.matmul(a1[:, j * C:(j + 1) * C], hT[:, j, :], wv_s[:], start=True, stop=True)
                    last.then_inc(S["proj"], 1)

                def term1(j):
                    pe.wait_ge(S["mask"], g + 1)
                    if j < 2:
                        pe.wait_ge(S["hE"], 2 * g + 2)
                    else:
                        pe.wait_ge(S["t"], 4 * g + j - 1)
                    ps = gp[j % 2]
                    pe.matmul(ps[:].rearrange("p (h l) -> p h l", h=NH), identb[:],
                              mask[:, j, :].unsqueeze(1).broadcast_to([L, NH, L]), start=True, stop=False)
                    for h in range(NH):
                        last = pe.matmul(ps[:, h * L:(h + 1) * L], wd[:, h, :], xnT[:, j, :], start=False, stop=h == NH - 1)
                    last.then_inc(S["P_ps"], 1)

                def score2(j):
                    if j == 0:
                        pe.wait_ge(S["qT"], a + 1)
                        pe.wait_ge(S["kd"], 2 * a + 2)
                        pe.wait_ge(S["kp"], 2 * a + 2)
                    else:
                        pe.wait_ge(S["e2"], 4 * a + j)
                    pe.matmul(a0[:].rearrange("p (h l) -> p h l", h=NH), identb[:],
                              causal[:].unsqueeze(1).broadcast_to([L, NH, L]), start=True, stop=False)
                    pe.matmul(a0[:], qT[:, j, :], kbd[:, j].rearrange("c h l -> c (h l)"), start=False, stop=True).then_inc(S["s_ps"], 1)

                def probs1(j):
                    pe.wait_ge(S["e1"], 4 * g + j + 1)
                    if late(g, 1) or j:
                        pe.wait_ge(S["pT1"], 4 * g + j)
                    flip(g2, p1[j % 2]).then_inc(S["pT1_ps"], 1)

                def probs2(j):
                    pe.wait_ge(S["e2"], 4 * a + j + 1)
                    if j:
                        pe.wait_ge(S["pT2"], 4 * a + j)
                    else:
                        pe.wait_ge(S["vE"], a + 1)
                    flip(a1, p2[j % 2]).then_inc(S["pT2_ps"], 1)

                def values1(j):
                    pe.wait_ge(S["pT1"], 4 * g + j + 1)
                    if j:
                        pe.wait_ge(S["og"], 4 * g + j)
                    for h in range(NH):
                        o = h * (GW - SKEW)
                        last = pe.matmul(g3[:, h * 128:(h + 1) * 128], pT1[j % 2][:, h, :], hE[:, j, o:o + 128], start=True, stop=True)
                    last.then_inc(S["pv1"], 1)

                def values2(j):
                    pe.wait_ge(S["pT2"], 4 * a + j + 1)
                    if j:
                        pe.wait_ge(S["y"], 4 * a + j)
                    else:
                        pe.wait_ge(S["ka"], a + 1)
                    for h in range(NH):
                        o = h * (HW - SKEW)
                        last = pe.matmul(a3[:, h * 128:(h + 1) * 128], pT2[j % 2][:, h, :], vE[:, j, o:o + 128], start=True, stop=True)
                    last.then_inc(S["pv2"], 1)

                def f_():
                    pe.wait_ge(S["fx"], 4 * t + 4)
                    flip(t2, fx[0][p]).then_inc(S["fT_ps"], 1)

                def lg_():
                    pe.wait_ge(S["fT"], t + 1)
                    for j in range(GB):
                        last = pe.matmul(t2[:, j * 128:(j + 1) * 128], fT[:, j, :], rout[:], start=True, stop=True)
                    last.then_inc(S["lg_ps"], 1)

                def rank():
                    pe.wait_ge(S["route"], ROUTE * t + 13)
                    for j in range(GB + 1):
                        o = t2[:, j * NE:(j + 1) * NE]
                        if j < GB:
                            last = pe.matmul(o, before[:], ohb[:, j, :], start=True, stop=j == 0)
                        for i in range(j):
                            last = pe.matmul(o, onesb[:], ohb[:, i, :], start=j == GB and i == 0, stop=i == j - 1)
                    last.then_inc(S["rank_ps"], 1)

                return {"yT": yT_, "xn": xn_, "hN": hN_, "wo": wo_, "h": h_, "q": q_, "k": k_, "kr": kr_, "v": v_, "f": f_, "lg": lg_,
                        "rank": rank, "p1": term1, "s2": score2, "o1": probs1, "o2": probs2, "v1": values1, "v2": values2}

            phase1(pe, steps)

            pe.wait_ge(S["wscale"], 2)
            pe.wait_ge(S["table"], 1)

            def turn_x(k, r):
                pe.wait_ge(S[f"xq{r}"], 16 // RING * (k - r) + 16)
                if late(k, 1):
                    pe.wait_ge(S["xT"], k)
                pe.transpose(x_p[:, 0:128], xt[r][:, 0:C], ident[:]).then_inc(S["xtr"], 1)

            def up(w, ps, k, q, e, s, used):
                if late(k, 2):
                    pe.wait_ge(S[used], k - 1)
                pe.matmul(ps[q][:, 0:HID], xT[q][:], w[:, bass.ds(e, 1), :].rearrange("c a n -> c (a n)"),
                          start=True, stop=True).then_inc(S[s], 1)

            def turn_h(k, q):
                pe.wait_ge(S["hu"], k + 1)
                if late(k, 1):
                    pe.wait_ge(S["hsT"], k)
                for c, (o, n) in enumerate(HC):
                    last = pe.transpose(hs_p[0:n, c * 128:(c + 1) * 128], hu[q][:, o:o + n], ident[:])
                last.then_inc(S["htr"], 1)

            def down(k, q, e):
                pe.wait_ge(S["hsT"], k + 1)
                if late(k, 2):
                    pe.wait_ge(S["ys"], k - 1)
                for c, (o, n) in enumerate(HC):
                    last = pe.matmul(y_p[q][:, 0:C], hsT[q][0:n, c, :], w2_s[0:n, bass.ds(e, 1), c, :].rearrange("p a c -> p (a c)"),
                                     start=c == 0, stop=c == 2)
                last.then_inc(S["yp"], 1)

            def expert(k):
                return pe.value_load(exi[0:1, bass.ds(k, 1)], min_val=0, max_val=NE - 1)

            def ring(k, first=False, last=False):
                e = {n: expert(k + n) for n in ((0,) if first else (-2, -1, 0))}
                for r in range(RING):
                    q = r % 2
                    if not (last and r == RING - 1):
                        turn_x(k + r + 1, (r + 1) % RING)
                    pe.wait_ge(S["xT"], k + r + 1)
                    up(w1_s, h1_p, k + r, q, e[r], "h1", "sg")
                    up(w3_s, h3_p, k + r, q, e[r], "h3", "hu")
                    if r + 1 < RING:
                        e[r + 1] = expert(k + r + 1)
                    if r >= 1 or not first:
                        turn_h(k + r - 1, 1 - q)
                    if r >= 2 or not first:
                        down(k + r - 2, q, e[r - 2])
                return e

            turn_x(0, 0)
            ring(0, first=True)
            with pe.Fori(1, NT // RING - 1) as i:
                ring(i * RING)
            e = ring(NT - RING, last=True)
            turn_h(NT - 1, 1)
            down(NT - 2, 0, e[RING - 2])
            down(NT - 1, 1, e[RING - 1])


def kernel(**inputs):
    import concourse.bacc as bacc
    from concourse.bass_utils import run_bass_kernel_spmd

    a = {k.replace("L0_", ""): np.asarray(v) for k, v in inputs.items()}
    tb = tables()
    wqh = a["ffn_wq"].reshape(NH, HD, C)
    wkh = np.repeat(a["ffn_wk"].reshape(NH // 2, HD, C), 2, 0)
    wvh = np.repeat(a["ffn_wv"].reshape(NH // 2, HD, C), 2, 0)

    def turned(w):
        return np.concatenate([w[:, HD // 2:], w[:, :HD // 2]], 1)

    def cols(w):
        return w.reshape(C, C).T

    arrays = {
        "x": a["x"], "adj": a["adj"], "W": a["gnn_W"], "WT": a["gnn_W"].T,
        "att_src": a["gnn_att_src"].reshape(NH, HD, 1), "att_dst": a["gnn_att_dst"].reshape(NH, HD, 1),
        "ln1": a["ffn_ln1_w"], "ln2": a["ffn_ln2_w"], "wq": cols(wqh), "wqr": cols(turned(wqh)),
        "wk": cols(wkh), "wkr": cols(turned(wkh)), "wv": cols(wvh), "wo": a["ffn_wo"].T, "router": a["ffn_router_w"].T,
        "w1": a["ffn_w1"].transpose(2, 0, 1), "w3": a["ffn_w3"].transpose(2, 0, 1), "w2": a["ffn_w2"].transpose(0, 2, 1),
        "rope_h": tb["rope"], "ident_h": tb["ident"], "causal_h": tb["causal"], "before_h": tb["before"],
        "small_h": tb["small"], "tileno_h": tb["tileno"],
    }
    arrays = {"in_" + k: np.ascontiguousarray(v) for k, v in arrays.items()}
    nc = bacc.Bacc("TRN2", target_bir_lowering=False, num_devices=1)
    args = [nc.dram_tensor(k, v.shape, mybir.dt.from_np(v.dtype), kind="ExternalInput").ap() for k, v in arrays.items()]
    out = nc.dram_tensor("out_0", (B, L, C), F32, kind="ExternalOutput").ap()
    gnn_moe_block(nc, *args, out)
    r = run_bass_kernel_spmd(nc, [arrays], core_ids=[0])
    return r.results[0]["out_0"]
```
